# Optimizing a Trainium2 kernel written in Bass

```python
import numpy as np
import jax
import jax.numpy as jnp

def _softmax(x, axis=-1):
    return jax.nn.softmax(x, axis=axis)

def _gelu(x):
    return jax.nn.gelu(x, approximate=True)

def _silu(x):
    return jax.nn.silu(x)

def _sigmoid(x):
    return jax.nn.sigmoid(x)

def _layernorm(x, axis=-1, eps=1e-05):
    m = jnp.mean(x, axis=axis, keepdims=True)
    v = jnp.var(x, axis=axis, keepdims=True)
    return (x - m) / jnp.sqrt(v + eps)

def _scatter_add(tgt, idx, src, axis=0):
    return tgt.at[idx].add(src)

def _segment_sum(src, seg, n):
    return jax.ops.segment_sum(src, seg, n)
kernel_name = 'mk_xattn_seq_d1_seqx_r2_543892'

def setup_inputs(seed: int=0):
    np.random.seed(seed)
    _w = jnp.asarray

    def _rec_inputs():
        import jax
        import jax.numpy as jnp
        _rk = jax.random.key(seed)
        x = -0.0001548 + 1 * jax.random.normal(jax.random.fold_in(_rk, 1), (2, 1024, 640), jnp.float32)
        _lenS = 1024 - jax.random.randint(jax.random.fold_in(_rk, 7), (2,), 0, max(1, 1024 // 4) + 1, jnp.int32)
        _lenS2 = 2048 - jax.random.randint(jax.random.fold_in(_rk, 8), (2,), 0, max(1, 2048 // 4) + 1, jnp.int32)
        _ctx_768P = jax.random.normal(jax.random.fold_in(_rk, 11), (2, 16, 384), jnp.float32)
        _ctx_768c = jax.random.dirichlet(jax.random.fold_in(_rk, 511), 0.3 * jnp.ones((16,), jnp.float32), (2, 2048))
        _ctx_768t = jnp.einsum('bsk,bkd->bsd', _ctx_768c, _ctx_768P)
        _ctx_768t = _ctx_768t * jax.lax.rsqrt(jnp.mean(jnp.square(_ctx_768t)) + 1e-12) * 0.953939
        ctx_768 = 0.00141353 + 0.998943 * (_ctx_768t + 0.3 * jax.random.normal(jax.random.fold_in(_rk, 611), (2, 2048, 384), jnp.float32))
        return (x, ctx_768)
    x, ctx_768 = _rec_inputs()

    def _L0_xattn_setup():
        import jax, jax.numpy as jnp
        import numpy as np
        HEADS = 8
        NUM_TOKENS = 4
        CROSS_ATTENTION_DIM = 384

        def _mha(q, k, v, heads=HEADS):
            B, Sq, H = q.shape
            Sk = k.shape[1]
            d = H // heads
            qh = q.reshape(B, Sq, heads, d).transpose(0, 2, 1, 3)
            kh = k.reshape(B, Sk, heads, d).transpose(0, 2, 1, 3)
            vh = v.reshape(B, Sk, heads, d).transpose(0, 2, 1, 3)
            scores = jnp.einsum('bhqd,bhkd->bhqk', qh, kh) * jnp.asarray(d, q.dtype) ** (-0.5)
            probs = jax.nn.softmax(scores, axis=-1)
            out = jnp.einsum('bhqk,bhkd->bhqd', probs, vh)
            return out.transpose(0, 2, 1, 3).reshape(B, Sq, H)
        key = jax.random.key(seed)
        ks = jax.random.split(key, 10)
        B, S, H, CAD, T = (4, 512, 640, CROSS_ATTENTION_DIM, NUM_TOKENS)
        sc = 0.02
        return {'hidden_states': jax.random.normal(ks[0], (B, S, H), jnp.float32), 'encoder_hidden_states': jax.random.normal(ks[1], (B, 77 + T, CAD), jnp.float32), 'Wq': jax.random.normal(ks[2], (H, H), jnp.float32) * sc, 'Wk': jax.random.normal(ks[3], (CAD, H), jnp.float32) * sc, 'Wv': jax.random.normal(ks[4], (CAD, H), jnp.float32) * sc, 'Wq_ca': jax.random.normal(ks[5], (T, H), jnp.float32) * sc, 'Wk_ca': jax.random.normal(ks[6], (CAD, H), jnp.float32) * sc, 'Wv_ca': jax.random.normal(ks[7], (CAD, H), jnp.float32) * sc, 'Wout': jax.random.normal(ks[8], (H, H), jnp.float32) * sc, 'b_out': jnp.zeros((H,), jnp.float32)}
    _L0_xattn_all = _L0_xattn_setup()
    _L0_xattn_in = {k: v for k, v in _L0_xattn_all.items() if k in ('Wq', 'Wk', 'Wv', 'Wq_ca', 'Wk_ca', 'Wv_ca', 'Wout', 'b_out')}
    del _L0_xattn_all
    return {'x': x, 'ctx_768': ctx_768, 'L0_xattn_Wq': _L0_xattn_in['Wq'], 'L0_xattn_Wk': _L0_xattn_in['Wk'], 'L0_xattn_Wv': _L0_xattn_in['Wv'], 'L0_xattn_Wq_ca': _L0_xattn_in['Wq_ca'], 'L0_xattn_Wk_ca': _L0_xattn_in['Wk_ca'], 'L0_xattn_Wv_ca': _L0_xattn_in['Wv_ca'], 'L0_xattn_Wout': _L0_xattn_in['Wout'], 'L0_xattn_b_out': _L0_xattn_in['b_out']}

def reference(x, ctx_768, L0_xattn_Wq, L0_xattn_Wk, L0_xattn_Wv, L0_xattn_Wq_ca, L0_xattn_Wk_ca, L0_xattn_Wv_ca, L0_xattn_Wout, L0_xattn_b_out):
    import jax
    import jax.numpy as jnp

    def _L0_xattn_ref(hidden_states, encoder_hidden_states, Wq, Wk, Wv, Wq_ca, Wk_ca, Wv_ca, Wout, b_out):
        import jax, jax.numpy as jnp
        import numpy as np
        HEADS = 8
        NUM_TOKENS = 4
        CROSS_ATTENTION_DIM = 384

        def _mha(q, k, v, heads=HEADS):
            B, Sq, H = q.shape
            Sk = k.shape[1]
            d = H // heads
            qh = q.reshape(B, Sq, heads, d).transpose(0, 2, 1, 3)
            kh = k.reshape(B, Sk, heads, d).transpose(0, 2, 1, 3)
            vh = v.reshape(B, Sk, heads, d).transpose(0, 2, 1, 3)
            scores = jnp.einsum('bhqd,bhkd->bhqk', qh, kh) * jnp.asarray(d, q.dtype) ** (-0.5)
            probs = jax.nn.softmax(scores, axis=-1)
            out = jnp.einsum('bhqk,bhkd->bhqd', probs, vh)
            return out.transpose(0, 2, 1, 3).reshape(B, Sq, H)
        residual = hidden_states
        unet_size = residual.shape[1]
        end_pos = encoder_hidden_states.shape[1] - NUM_TOKENS
        enc = encoder_hidden_states[:, :end_pos, :]
        ca = encoder_hidden_states[:, end_pos:, :]
        query = hidden_states @ Wq
        keyt = enc @ Wk
        valt = enc @ Wv
        hs = _mha(query, keyt, valt)
        ca_q1 = jnp.einsum('btc,th->bch', ca, Wq_ca)
        indices = np.linspace(0, CROSS_ATTENTION_DIM - 1, unet_size).astype(np.int64)
        ca_q1 = ca_q1[:, indices, :]
        ca_hs1 = _mha(ca_q1, residual, residual)
        ca_q2 = ca_hs1 @ Wq
        ca_k2 = ca @ Wk_ca
        ca_v2 = ca @ Wv_ca
        ca_hs2 = _mha(ca_q2, ca_k2, ca_v2)
        out = hs + ca_hs2
        out = out @ Wout + b_out
        out = out + residual
        return out
    x = _L0_xattn_ref(x, ctx_768, L0_xattn_Wq, L0_xattn_Wk, L0_xattn_Wv, L0_xattn_Wq_ca, L0_xattn_Wk_ca, L0_xattn_Wv_ca, L0_xattn_Wout, L0_xattn_b_out)
    return x

_drawn_inputs = setup_inputs


def setup_inputs(seed=0):
    import zlib

    import numpy as np

    out = dict(_drawn_inputs(seed))
    spreads = {'L0_xattn_b_out': (0.0, 0.1)}
    factors = {'L0_xattn_Wq': 8.0, 'L0_xattn_Wk': 8.0, 'L0_xattn_Wq_ca': 8.0, 'L0_xattn_Wk_ca': 8.0}
    for name, (base, spread) in spreads.items():
        noise = np.random.default_rng([zlib.crc32(name.encode()), seed]).standard_normal(out[name].shape)
        drawn = base * np.exp(spread * noise) if base else spread * noise
        out[name] = jnp.asarray(drawn.astype(out[name].dtype))
    for name, factor in factors.items():
        out[name] = (out[name] * factor).astype(out[name].dtype)
    return out
```

```python
from contextlib import ExitStack

import concourse.bass as bass
from concourse import mybir
import numpy as np

F32 = mybir.dt.float32
F32R = mybir.dt.float32r
ALU = mybir.AluOpType
ACT = mybir.ActivationFunctionType
AX = mybir.AxisListType.X

P = 128
B, SQ, HID = 2, 1024, 640
SKV, CD, NT = 2048, 384, 4
SK = SKV - NT
NH = 8
D = HID // NH
SCALE = float(D) ** -0.5
MC, KC = HID // P, CD // P
HT = NH * NT
CH = 512
HALF = HID // 2
KT = SKV // P
LASTK = SK - (KT - 1) * P
ST = SQ // P
G = B * NH
DA = D + 1
LO_A = P - D
LO_B = D - LO_A
SHIFT = D + LO_B


def gather_index():
    return np.linspace(0, CD - 1, SQ).astype(np.int64)


def products(a, b):
    return ((a[0], b[0]), (a[0], b[1]), (a[1], b[0]))


class Scope:
    def __init__(self, nc, stack):
        self.nc, self.stack = nc, stack

    def sb(self, name, shape, dt=F32):
        return self.stack.enter_context(self.nc.sbuf_tensor(name, shape, dt))

    def psum(self, name, shape, dt=F32):
        return self.stack.enter_context(self.nc.psum_tensor(name, shape, dt))

    def sem(self, name):
        return self.stack.enter_context(self.nc.semaphore(name))


def prepare(nc, kept, w, d):
    with ExitStack() as stack:
        s = Scope(nc, stack)
        wqT = s.sb("wqT", [P, MC, HID])
        wout = s.sb("wout_f", [P, MC, HID])
        wkca = s.sb("wkca", [P, KC, HID])
        wvca = s.sb("wvca", [P, KC, HID])
        caT = s.sb("caT", [P, KC, B * NT])
        mask = s.sb("mask", [P, MC, NH])
        stage = {n: s.sb(f"stage_{n}", list(w[n][0].shape)) for n in ("wqca",)}
        big = s.sb("stage_big", [P, MC, HID])
        k2 = s.sb("k2", [P, MC, B * NT])
        v2 = s.sb("v2", [P, MC, B * NT])
        k2bd = s.sb("k2bd", [P, MC, B, NH, NT])
        v2bd = s.sb("v2bd", [P, MC, B, NH, NT])
        k2_ps = s.psum("k2_ps", [P, MC, B * NT])
        v2_ps = s.psum("v2_ps", [P, MC, B * NT])
        wk2_ps = s.psum("wk2_ps", [D, NH, B, HT])
        vw_ps = [s.psum(f"vw_ps{b}", [HT, 2, CH]) for b in range(B)]

        small_in = s.sem("prep_small_in")
        wqT_in = s.sem("prep_wqT_in")
        wout_in = s.sem("prep_wout_in")
        wk2_in = s.sem("prep_wk2_in")
        w_in = [s.sem(f"prep_w_in{n}") for n in range(4)]
        hi_done, lo_done = s.sem("prep_hi"), s.sem("prep_lo")
        kv_full = s.sem("prep_kv_full")
        kv_copied = s.sem("prep_kv_copied")
        bd_done = s.sem("prep_bd_done")
        wk2_full = s.sem("prep_wk2_full")
        wk2_done = s.sem("prep_wk2_done")
        vw_full = s.sem("prep_vw_full")
        vw_done = s.sem("prep_vw_done")
        order = ("wk", "wv", "wq", "wqca")
        rows = lambda a: a.rearrange("(m p) n -> p m n", p=P)

        with nc.Block() as block:
            @block.sync
            def _(sp):
                sp.dma_start(wkca[:], rows(d["wkca"])).then_inc(small_in, 16)
                sp.dma_start(caT[:], rows(d["caT"])).then_inc(small_in, 16)
                sp.dma_start(wvca[:], rows(d["wvca"])).then_inc(small_in, 16)
                sp.dma_start(mask[:], rows(d["mask"])).then_inc(small_in, 16)
                sp.dma_start(kept["wk2"][:], d["wk2_frame"]).then_inc(wk2_in, 16)
                sp.dma_start(wqT[:], rows(d["wqT"])).then_inc(wqT_in, 16)
                sp.dma_start(wout[:], rows(d["wout"])).then_inc(wout_in, 16)
                for n, name in enumerate(order):
                    src = rows(d[name])
                    dst = stage[name] if name in stage else big[:, 0:src.shape[1], :]
                    if n:
                        sp.wait_ge(lo_done, n)
                    sp.dma_start(dst[:] if name in stage else dst, src).then_inc(w_in[n], 16)

            @block.scalar
            def _(act):
                for n, name in enumerate(order):
                    hi, _lo = w[name]
                    src = stage[name][:] if name in stage else big[:, 0:hi.shape[1], :]
                    act.wait_ge(w_in[n], 16)
                    act.activation(hi[:], src, ACT.Copy).then_inc(hi_done, 1)
                for b in range(B):
                    act.wait_ge(vw_full, b + 1)
                    act.activation(kept["vw"][:, b, :].rearrange("p (u n) -> p u n", u=2),
                                   vw_ps[b][:, :, 0:HALF], ACT.Copy).then_inc(vw_done, 1)
                act.wait_ge(vw_done, B)

            @block.vector
            def _(dve):
                dve.wait_ge(kv_full, 1)
                dve.tensor_copy(k2[:], k2_ps[:]).then_inc(kv_copied, 1)
                dve.wait_ge(kv_full, 2)
                dve.tensor_copy(v2[:], v2_ps[:]).then_inc(kv_copied, 1)
                dve.wait_ge(small_in, 64)
                dve.wait_ge(kv_copied, 2)
                for src, dst in ((k2, k2bd), (v2, v2bd)):
                    for b in range(B):
                        tok = src[:, :, None, b * NT:(b + 1) * NT].to_broadcast([P, MC, NH, NT])
                        own = mask[:, :, :, None].to_broadcast([P, MC, NH, NT])
                        dve.tensor_tensor(dst[:, :, b], tok, own, ALU.mult).then_inc(bd_done, 1)
                for n, name in enumerate(order):
                    hi, lo = w[name]
                    src = stage[name][:] if name in stage else big[:, 0:hi.shape[1], :]
                    dve.wait_ge(hi_done, n + 1)
                    dve.tensor_tensor(lo[:], src, hi[:].bitcast(F32), ALU.subtract).then_inc(lo_done, 1)
                dve.wait_ge(wk2_full, 1)
                dve.wait_ge(wk2_in, 16)
                for b in range(B):
                    dve.tensor_copy(kept["wk2"][0:D, b, :, 0:HT], wk2_ps[:, :, b, :]).then_inc(wk2_done, 1)

            @block.tensor
            def _(pe):
                pe.wait_ge(small_in, 64)
                for wt, ps in ((wkca, k2_ps), (wvca, v2_ps)):
                    for m in range(MC):
                        for c in range(KC):
                            mm = pe.matmul(ps[:, m, :], wt[:, c, m * P:(m + 1) * P], caT[:, c, :],
                                           start=c == 0, stop=c == KC - 1)
                    mm.then_inc(kv_full, 1)
                pe.wait_ge(wqT_in, 16)
                pe.wait_ge(bd_done, 2 * B)
                for h in range(NH):
                    for m in range(MC):
                        mm = pe.matmul(wk2_ps[:, h].rearrange("p b n -> p (b n)"),
                                       wqT[:, m, h * D:(h + 1) * D],
                                       k2bd[:, m].rearrange("p b h t -> p (b h t)"),
                                       start=m == 0, stop=m == MC - 1)
                mm.then_inc(wk2_full, 1)
                pe.wait_ge(wout_in, 16)
                for b in range(B):
                    for u in range(2):
                        for m in range(MC):
                            mm = pe.matmul(vw_ps[b][:, u, 0:HALF],
                                           v2bd[:, m, b].rearrange("p h t -> p (h t)"),
                                           wout[:, m, u * HALF:(u + 1) * HALF],
                                           start=m == 0, stop=m == MC - 1)
                    mm.then_inc(vw_full, 1)


def project(nc, kept, w, d, scratch):
    NS = SKV // CH
    NQ = SQ // CH
    RING = 3
    with ExitStack() as stack:
        s = Scope(nc, stack)
        ctx_f = [s.sb(f"ctx_f{i}", [P, 1, KC, CH]) for i in range(2)]
        ctx_s = [(s.sb(f"ctx_hi{i}", [P, KC, CH], F32R), s.sb(f"ctx_lo{i}", [P, KC, CH], F32R)) for i in range(2)]
        x_f = s.sb("x_f", [P, 1, MC, CH])
        x_s = (s.sb("x_hi", [P, MC, CH], F32R), s.sb("x_lo", [P, MC, CH], F32R))
        ring = [(s.sb(f"out_hi{i}", [P, CH], F32R), s.sb(f"out_lo{i}", [P, CH], F32R)) for i in range(RING)]
        v_t = [s.sb(f"v_t{i}", [P, NH, CH // P, D]) for i in range(2)]
        banks = [s.psum(f"bank{i}", [P, CH]) for i in range(8)]
        u_all = kept["u"]

        ctx_in = [s.sem(f"pj_ctx_in{i}") for i in range(2)]
        ctx_hi, ctx_lo = s.sem("pj_ctx_hi"), s.sem("pj_ctx_lo")
        x_in, x_hi, x_lo = s.sem("pj_x_in"), s.sem("pj_x_hi"), s.sem("pj_x_lo")
        full, hi_done, done = s.sem("pj_full"), s.sem("pj_hi"), s.sem("pj_done")
        ring_out = [s.sem(f"pj_ring_out{i}") for i in range(RING)]
        v_out = [s.sem(f"pj_v_out{i}") for i in range(2)]

        jobs = []
        for c in range(NS):
            jobs += [("k", c, m) for m in range(MC)]
            jobs += [("v", c, (t, u)) for t in range(4) for u in range(2)]
            if c % 2:
                jobs += [("q", c // 2, m) for m in range(MC)] + [("u", c // 2, 0)]
        NJ = len(jobs)
        assert NJ % 8 == 0
        split_jobs = [j for j in jobs if j[0] != "v"]
        ring_jobs = [j for j in jobs if j[0] in "kq"]
        last = {(kind, c): n for n, (kind, c, _) in enumerate(jobs)}

        def read_ctx(c):
            return last["v", c] + 1 + NJ if c >= 0 else last["v", c + NS] + 1

        def read_x(c):
            return last["u", c] + 1 + NJ if c >= 0 else last["u", c + NQ] + 1

        NSP, NR = len(split_jobs), len(ring_jobs)
        assert NR % RING == 0

        ctxT = d["ctxT"].rearrange("b (m p) s -> p b m s", p=P)
        xT = d["xT"].rearrange("b (m p) s -> p b m s", p=P)

        with nc.Block() as block:
            @block.gpsimd
            def _(pool):
                pool.sem_inc(ctx_lo, 2)
                pool.sem_inc(x_lo, 1)
                pool.memset(u_all[3 * HT:3 * HT + 1, :].bitcast(F32), 1.0).then_inc(kept["u_ones"], 1)
                with pool.Fori(0, B) as b:
                    for c in range(NS):
                        pool.wait_ge(ctx_lo, b * NS + c + 1)
                        pool.dma_start(ctx_f[c % 2][:], ctxT[:, bass.ds(b, 1), :, c * CH:(c + 1) * CH]
                                       ).then_inc(ctx_in[c % 2], 16)
                        if c % 2 == 0:
                            q = c // 2
                            pool.wait_ge(x_lo, b * NQ + q + 1)
                            pool.dma_start(x_f[:], xT[:, bass.ds(b, 1), :, q * CH:(q + 1) * CH]
                                           ).then_inc(x_in, 16)

            @block.sync
            def _(sp):
                with sp.Fori(0, B) as b:
                    nr = ns = 0
                    for n, (kind, c, m) in enumerate(jobs):
                        if kind in "kq":
                            hi, lo = ring[nr % RING]
                            to = scratch["kh"], scratch["kl"]
                            if kind == "q":
                                to = scratch["qh"], scratch["ql"]
                            at = (bass.ds(b * HID + m * P, P), slice(c * CH, (c + 1) * CH))
                            sp.wait_ge(hi_done, b * NSP + ns + 1)
                            sp.dma_start(to[0][at], hi[:].bitcast(F32)).then_inc(ring_out[nr % RING], 16)
                            sp.wait_ge(done, b * NJ + n + 1 + 8)
                            sp.dma_start(to[1][at], lo[:].bitcast(F32)).then_inc(ring_out[nr % RING], 16)
                            nr += 1
                        if kind != "v":
                            ns += 1
                        if kind == "v" and m == (3, 1):
                            sp.wait_ge(done, b * NJ + n + 1 + 8)
                            sp.dma_start(scratch["v"][bass.ds(b * NH, NH), :, c * 4 * D:(c + 1) * 4 * D]
                                         .rearrange("h p n -> p h n"),
                                         v_t[c % 2][:].rearrange("p h t d -> p h (t d)")).then_inc(v_out[c % 2], 16)
                for i in range(RING):
                    sp.wait_ge(ring_out[i], 32 + B * NR // RING * 32)
                for i in range(2):
                    sp.wait_ge(v_out[i], 16 + B * NS // 2 * 16)

            @block.scalar
            def _(act):
                for i in range(RING):
                    act.sem_inc(ring_out[i], 32)

                def split_ctx(b, c):
                    act.wait_ge(ctx_in[c % 2], (b * (NS // 2) + c // 2 + 1) * 16)
                    act.wait_ge(full, b * NJ + read_ctx(c - 2))
                    act.activation(ctx_s[c % 2][0][:], ctx_f[c % 2][:, 0], ACT.Copy).then_inc(ctx_hi, 1)

                def split_x(b, q):
                    act.wait_ge(x_in, (b * NQ + q + 1) * 16)
                    act.wait_ge(full, b * NJ + read_x(q - 1))
                    act.activation(x_s[0][:], x_f[:, 0], ACT.Copy).then_inc(x_hi, 1)

                with act.Fori(0, B) as b:
                    nr = 0
                    split_ctx(b, 0)
                    split_x(b, 0)
                    for n, (kind, c, m) in enumerate(jobs):
                        if kind == "k" and m == 0 and c < NS - 1:
                            split_ctx(b, c + 1)
                        if kind == "k" and m == 0 and c == 2:
                            split_x(b, 1)
                        if kind == "v":
                            continue
                        act.wait_ge(full, b * NJ + n + 1 + NJ)
                        if kind == "u":
                            dst = u_all[0:3 * HT, bass.ds(b * SQ + c * CH, CH)]
                            act.activation(dst, banks[n % 8][0:3 * HT, :], ACT.Copy).then_inc(hi_done, 1)
                        else:
                            act.wait_ge(ring_out[nr % RING], (b * (NR // RING) + nr // RING + 1) * 32)
                            act.activation(ring[nr % RING][0][:], banks[n % 8][:], ACT.Copy).then_inc(hi_done, 1)
                            nr += 1

            @block.vector
            def _(dve):
                for i in range(2):
                    dve.sem_inc(v_out[i], 16)

                def split_ctx(b, c):
                    dve.wait_ge(ctx_hi, b * NS + c + 1)
                    hi, lo = ctx_s[c % 2]
                    dve.tensor_tensor(lo[:], ctx_f[c % 2][:, 0], hi[:].bitcast(F32), ALU.subtract).then_inc(ctx_lo, 1)

                def split_x(b, q):
                    dve.wait_ge(x_hi, b * NQ + q + 1)
                    hi, lo = x_s
                    dve.tensor_tensor(lo[:], x_f[:, 0], hi[:].bitcast(F32), ALU.subtract).then_inc(x_lo, 1)

                with dve.Fori(0, B) as b:
                    nr = ns = 0
                    split_ctx(b, 0)
                    split_x(b, 0)
                    for n, (kind, c, m) in enumerate(jobs):
                        if kind == "k" and m == 0 and c < NS - 1:
                            split_ctx(b, c + 1)
                        if kind == "k" and m == 0 and c == 2:
                            split_x(b, 1)
                        bank = banks[n % 8]
                        if kind == "v":
                            t, u = m
                            dve.wait_ge(full, b * NJ + n + 1 + NJ)
                            if t == 0 and u == 0:
                                dve.wait_ge(v_out[c % 2], (b * (NS // 2) + c // 2 + 1) * 16)
                            dve.tensor_copy(v_t[c % 2][:, u * 4:(u + 1) * 4, t, :],
                                            bank[:, 0:HALF].rearrange("p (h d) -> p h d", d=D)).then_inc(done, 1)
                            continue
                        dve.wait_ge(hi_done, b * NSP + ns + 1)
                        if kind == "u":
                            dst = u_all[2 * HT:3 * HT, bass.ds(b * SQ + c * CH, CH)]
                            dve.tensor_tensor(dst, bank[2 * HT:3 * HT, :], dst.bitcast(F32),
                                              ALU.subtract).then_inc(done, 1)
                        else:
                            hi, lo = ring[nr % RING]
                            dve.tensor_tensor(lo[:], bank[:], hi[:].bitcast(F32), ALU.subtract).then_inc(done, 1)
                            nr += 1
                        ns += 1

            @block.tensor
            def _(pe):
                pe.sem_inc(done, 8)
                pe.sem_inc(full, NJ)
                with pe.Fori(0, B) as b:
                    for n, (kind, c, m) in enumerate(jobs):
                        bank = banks[n % 8]
                        if kind == "k" and m == 0:
                            pe.wait_ge(ctx_lo, b * NS + c + 1 + 2)
                        if kind == "q" and m == 0:
                            pe.wait_ge(x_lo, b * NQ + c + 1 + 1)
                        pe.wait_ge(done, b * NJ + n + 1)
                        nk = {"k": KC, "v": KC, "q": MC, "u": MC}[kind]
                        mm = None
                        for k in range(nk):
                            if kind == "k":
                                pairs = [(a[:, k, m * P:(m + 1) * P], y[:, k, :])
                                         for a, y in products(w["wk"], ctx_s[c % 2])]
                                to = bank[:]
                            elif kind == "v":
                                t, u = m
                                pairs = [(a[:, k, t * P:(t + 1) * P], y[:, k, u * HALF:(u + 1) * HALF])
                                         for a, y in products(ctx_s[c % 2], w["wv"])]
                                to = bank[:, 0:HALF]
                            elif kind == "q":
                                pairs = [(a[:, k, m * P:(m + 1) * P], y[:, k, :]) for a, y in products(w["wq"], x_s)]
                                to = bank[:]
                            else:
                                pairs = [(a[:, k, :], y[:, k, :]) for a, y in products(w["wqca"], x_s)]
                                to = bank[0:3 * HT, :]
                            for i, (a, y) in enumerate(pairs):
                                mm = pe.matmul(to, a, y, start=k == 0 and i == 0, stop=k == nk - 1 and i == 2)
                        mm.then_inc(full, 1)


def tokens(nc, kept, d):
    NI = 2 * NH * KC
    with ExitStack() as stack:
        s = Scope(nc, stack)
        ca_f = s.sb("ca_f", [P, NH * CD])
        ca = [s.sb(f"ca{b}", [P, NH * CD], F32R) for b in range(B)]
        xn = [s.sb(f"xn{b}", [P, ST, NH, DA]) for b in range(B)]
        onehot = s.sb("onehot", [P, SQ])
        part = s.sb("part", [P, B, NH, KC, 2])
        top = s.sb("top", [P, B, NH * KC])
        ntop = s.sb("ntop", [P, B, NH * KC], F32R)
        p1 = [s.sb(f"p1_{i}", [P, 2, CD]) for i in range(3)]
        raw = [s.sb(f"raw{i}", [DA, CD]) for i in range(2)]
        rden = s.sb("rden", [P, 2, KC])
        s2 = s.sb("s2", [P, B, KC, HT])
        t2 = s.sb("t2", [P, B, KC * NH])
        r2 = s.sb("r2", [P, B, KC * NH])
        p2 = s.sb("p2", [P, B, KC, HT])
        mx_ps = [s.psum(f"mx_ps{i}", [P, CH]) for i in range(2)]
        s_ps = [s.psum(f"s_ps{i}", [P, 2, CH]) for i in range(2)]
        acc_ps = s.psum("acc_ps", [DA, CH])
        t_ps = s.psum("t_ps", [P, KC, HT + 2])

        ca_in = [s.sem(f"tk_ca_in{b}") for b in range(B)]
        xn_in = [s.sem(f"tk_xn_in{b}") for b in range(B)]
        oh_in = s.sem("tk_onehot_in")
        xn_ones = s.sem("tk_xn_ones")
        ca_hi, ca_lo = s.sem("tk_ca_hi"), s.sem("tk_ca_lo")
        mx_full, mx_done = s.sem("tk_mx_full"), s.sem("tk_mx_done")
        top_done, ntop_done = s.sem("tk_top"), s.sem("tk_ntop")
        ntop_in = [s.sem(f"tk_ntop_in{b}") for b in range(B)]
        s_full, e_done, pv_done = s.sem("tk_s_full"), s.sem("tk_exp"), s.sem("tk_pv")
        raw_done, t_full = s.sem("tk_raw"), s.sem("tk_t_full")
        step = s.sem("tk_step")
        d2_done, e2_done, p2_done = s.sem("tk_d2"), s.sem("tk_e2"), s.sem("tk_p2")
        g_full, g_done = s.sem("tk_g_full"), s.sem("tk_g_done")

        idx = gather_index()
        spans = []
        for c in range(KC):
            q = np.flatnonzero(idx // P == c)
            lo, hi = int(q[0]), int(q[-1]) + 1
            cuts = [lo, CH, hi] if lo < CH < hi else [lo, hi]
            spans += [(c, a, z) for a, z in zip(cuts, cuts[1:])]
        K3 = 3 * HT
        pairs = ST // 2
        heads = [(b, h) for b in range(B) for h in range(NH)]
        per_head = NI // NH

        with nc.Block() as block:
            @block.sync
            def _(sp):
                xv = d["x"].rearrange("b (t p) (h d) -> b p t h d", p=P, d=D)
                for b in range(B):
                    if b:
                        sp.wait_ge(ca_lo, b)
                    sp.dma_start(ca_f[0:K3, :], d["caBD"][b]).then_inc(ca_in[b], 16)
                    for t in range(ST):
                        sp.dma_start(xn[b][:, t, :, 0:D], xv[b, :, t]).then_inc(xn_in[b], 16)
                sp.dma_start(onehot[:], d["onehot"]).then_inc(oh_in, 16)
                for b in range(B):
                    sp.wait_ge(ntop_done, b + 1)
                    for h in range(NH):
                        row = ca[b][K3:K3 + 1, h * CD:(h + 1) * CD].rearrange("o (p c) -> o p c", c=KC)
                        sp.dma_start(row.bitcast(F32), ntop[:, b, h * KC:(h + 1) * KC].bitcast(F32)
                                     ).then_inc(ntop_in[b], 16)

            @block.gpsimd
            def _(pool):
                for b in range(B):
                    pool.memset(xn[b][:, :, :, D:DA], 1.0).then_inc(xn_ones, 1)

            @block.scalar
            def _(act):
                def split(b):
                    act.wait_ge(ca_in[b], 16)
                    act.activation(ca[b][0:K3, :], ca_f[0:K3, :], ACT.Copy).then_inc(ca_hi, 1)

                def raw_out(n):
                    act.wait_ge(pv_done, (n + 1) * pairs)
                    if n >= 2:
                        act.wait_ge(t_full, n - 1)
                    act.activation(raw[n % 2][:], acc_ps[:, 0:CD], ACT.Copy).then_inc(raw_done, 1)

                split(0)
                split(1)
                for n, (b, h) in enumerate(heads):
                    for j in range(pairs):
                        k = n * pairs + j
                        act.wait_ge(s_full, k + 1)
                        if k >= 3:
                            act.wait_ge(pv_done, k - 2)
                        act.activation(p1[k % 3][:], s_ps[k % 2][:, :, 0:CD], ACT.Exp,
                                       scale=SCALE).then_inc(e_done, 1)
                        if j == 1 and n:
                            raw_out(n - 1)
                raw_out(len(heads) - 1)
                for b in range(B):
                    act.wait_ge(d2_done, b + 1)
                    act.activation(s2[:, b], s2[:, b], ACT.Exp, scale=SCALE).then_inc(e2_done, 1)

            @block.vector
            def _(dve):
                steps = [0]

                def chained(ins):
                    steps[0] += 1
                    ins.then_inc(step, 1)
                    dve.wait_ge(step, steps[0])

                def split(b):
                    dve.wait_ge(ca_hi, b + 1)
                    rows = slice(HT, 2 * HT)
                    dve.tensor_tensor(ca[b][rows, :], ca_f[rows, :], ca[b][rows, :].bitcast(F32),
                                      ALU.subtract).then_inc(ca_lo, 1)

                def piece(b, i):
                    n = b * NI + i
                    dve.wait_ge(mx_full, n + 1)
                    dst = part[:, b, i // per_head, i % per_head // 2, i % 2:i % 2 + 1]
                    dve.tensor_reduce(dst, mx_ps[n % 2][:], AX, ALU.max).then_inc(mx_done, 1)

                def maxima(b):
                    dve.wait_ge(mx_done, (b + 1) * NI)
                    dve.tensor_reduce(top[:, b, :], part[:, b].rearrange("p h c u -> p (h c) u"), AX,
                                      ALU.max).then_inc(top_done, 1)
                    dve.wait_ge(top_done, b + 1)
                    dve.tensor_scalar(ntop[:, b, :], top[:, b, :], -1.0, None, ALU.mult).then_inc(ntop_done, 1)

                def fold(n):
                    b, h = heads[n]
                    dve.wait_ge(t_full, n + 1)
                    chained(dve.reciprocal(rden[:, n % 2, :], t_ps[:, :, HT]))
                    for c in range(KC):
                        r = rden[:, n % 2, c:c + 1]
                        if h == 0:
                            chained(dve.tensor_scalar(s2[:, b, c, :], t_ps[:, c, 0:HT], r, None, ALU.mult))
                        else:
                            chained(dve.scalar_tensor_tensor(out=s2[:, b, c, :], in0=t_ps[:, c, 0:HT], scalar=r,
                                                             in1=s2[:, b, c, :], op0=ALU.mult, op1=ALU.add))

                def center(b):
                    v = s2[:, b].rearrange("p c (h t) -> p (c h) t", t=NT)
                    chained(dve.tensor_reduce(t2[:, b, :], v, AX, ALU.max))
                    dve.tensor_tensor(v, v, t2[:, b, :, None].to_broadcast([P, KC * NH, NT]),
                                      ALU.subtract).then_inc(d2_done, 1)

                def weigh(b):
                    v = s2[:, b].rearrange("p c (h t) -> p (c h) t", t=NT)
                    dve.wait_ge(e2_done, b + 1)
                    chained(dve.tensor_reduce(t2[:, b, :], v, AX, ALU.add))
                    chained(dve.reciprocal(r2[:, b, :], t2[:, b, :]))
                    dve.tensor_tensor(p2[:, b].rearrange("p c (h t) -> p (c h) t", t=NT), v,
                                      r2[:, b, :, None].to_broadcast([P, KC * NH, NT]), ALU.mult).then_inc(p2_done, 1)

                split(0)
                split(1)
                for i in range(NI):
                    piece(0, i)
                maxima(0)
                for n, (b, h) in enumerate(heads):
                    if b == 0:
                        for i in range(h * per_head, (h + 1) * per_head):
                            piece(1, i)
                        if h == NH - 1:
                            maxima(1)
                    if n:
                        fold(n - 1)
                fold(len(heads) - 1)
                for b in range(B):
                    center(b)
                for b in range(B):
                    weigh(b)
                for b in range(B):
                    dve.wait_ge(g_full, b + 1)
                    dve.tensor_copy(kept["p2g"][:, b, :], s_ps[b][0:HT].rearrange("p u n -> p (u n)")
                                    ).then_inc(g_done, 1)
                dve.wait_ge(g_done, B)

            @block.tensor
            def _(pe):
                def piece(b, i):
                    n = b * NI + i
                    h, c, u = i // per_head, i % per_head // 2, i % 2
                    if n >= 2:
                        pe.wait_ge(mx_done, n - 1)
                    pe.matmul(mx_ps[n % 2][:], ca[b][0:K3, h * CD + c:(h + 1) * CD:KC],
                              kept["u"][0:K3, b * SQ + u * CH:b * SQ + (u + 1) * CH],
                              start=True, stop=True).then_inc(mx_full, 1)

                def scores(k):
                    n, j = divmod(k, pairs)
                    b, h = heads[n]
                    if k % (NH * pairs) == 0:
                        pe.wait_ge(ntop_in[b], 16 * NH)
                    if k >= 2:
                        pe.wait_ge(e_done, k - 1)
                    for t in range(2):
                        st = 2 * j + t
                        mm = pe.matmul(s_ps[k % 2][:, t, 0:CD],
                                       kept["u"][0:K3 + 1, b * SQ + st * P:b * SQ + (st + 1) * P],
                                       ca[b][0:K3 + 1, h * CD:(h + 1) * CD], start=True, stop=True)
                    mm.then_inc(s_full, 1)

                def token_scores(n):
                    b, h = heads[n]
                    pe.wait_ge(raw_done, n + 1)
                    if n:
                        pe.wait_ge(step, 4 * n)
                    for c in range(KC):
                        mm = pe.matmul(t_ps[:, c, :], raw[n % 2][:, c * P:(c + 1) * P],
                                       kept["wk2"][:, b, h, :], start=True, stop=True)
                    mm.then_inc(t_full, 1)

                pe.wait_ge(kept["u_ones"], 1)
                pe.wait_ge(ca_lo, 1)
                for i in range(NI):
                    piece(0, i)
                pe.wait_ge(ca_lo, 2)
                total = len(heads) * pairs
                scores(0)
                for k in range(total):
                    n, j = divmod(k, pairs)
                    b, h = heads[n]
                    if k + 1 < total and (k + 1) % (NH * pairs):
                        scores(k + 1)
                    if b == 0:
                        for i in range(h * per_head, (h + 1) * per_head)[j * per_head // pairs:(j + 1) * per_head // pairs]:
                            piece(1, i)
                    if k == 0:
                        pe.wait_ge(xn_ones, B)
                    if k % (NH * pairs) == 0:
                        pe.wait_ge(xn_in[b], 16 * ST)
                    pe.wait_ge(e_done, k + 1)
                    if j == 0 and n:
                        pe.wait_ge(raw_done, n)
                    for t in range(2):
                        mm = pe.matmul(acc_ps[:, 0:CD], xn[b][:, 2 * j + t, h, :], p1[k % 3][:, t, :],
                                       start=j == 0 and t == 0, stop=j == pairs - 1 and t == 1)
                    mm.then_inc(pv_done, 1)
                    if k + 1 < total and (k + 1) % (NH * pairs) == 0:
                        scores(k + 1)
                    if j == 1 and n:
                        token_scores(n - 1)
                token_scores(len(heads) - 1)
                pe.wait_ge(oh_in, 16)
                for b in range(B):
                    pe.wait_ge(p2_done, b + 1)
                    for c, a, z in spans:
                        mm = pe.matmul(s_ps[b][0:HT, a // CH, a % CH:a % CH + z - a], p2[:, b, c, :],
                                       onehot[:, a:z], start=True, stop=True)
                    mm.then_inc(g_full, 1)


PB = 4
PF = 2
MXN = ST * SKV // CH
PIECES = (2, 3, 2, 3, 3, 2, 3, 3, 2, 3, 3, 3)
POOL_T = ()
SPLIT_AT = 1


def attend(nc, kept, scratch):
    with ExitStack() as stack:
        s = Scope(nc, stack)
        ka = [s.sb(f"ka{p}", [P, SKV], F32R) for p in range(2)]
        kb = [s.sb(f"kb{p}", [P, SKV], F32R) for p in range(2)]
        qa = [s.sb(f"qa{p}", [P, SQ], F32R) for p in range(2)]
        qb = [s.sb(f"qb{p}", [P, SQ], F32R) for p in range(2)]
        v_f = s.sb("v_f", [P, 1, KT * D])
        v_s = [(s.sb(f"v_hi{p}", [P, KT, DA], F32R), s.sb(f"v_lo{p}", [P, KT, DA], F32R)) for p in range(2)]
        prob = [s.sb(f"prob{i}", [P, SQ]) for i in range(PF)]
        ph = [s.sb(f"prob_hi{i}", [P, SQ], F32R) for i in range(PB)]
        pl = [s.sb(f"prob_lo{i}", [P, SQ], F32R) for i in range(PB)]
        mpart = s.sb("mpart", [P, 2, ST, SKV // CH])
        mtop = s.sb("mtop", [P, 2, ST])
        mneg = s.sb("mneg", [P, 2, ST], F32R)
        o_raw = [s.sb(f"o_raw{p}", [DA, SQ]) for p in range(2)]
        den = [s.sb(f"den{p}", [P, ST]) for p in range(2)]
        rden = [s.sb(f"rden{p}", [P, ST]) for p in range(2)]
        rbc = s.sb("rbc", [D, SQ])
        one = s.sb("one", [P, 1])
        s_ps = [s.psum(f"at_s_ps{i}", [P, SQ]) for i in range(2)]
        o_ps = s.psum("at_o_ps", [DA, SQ])
        mx_ps = [s.psum(f"at_mx_ps{i}", [P, CH]) for i in range(2)]

        qk_in = [s.sem(f"at_qk_in{p}") for p in range(2)]
        qkb_in = [s.sem(f"at_qkb_in{p}") for p in range(2)]
        neg_in = [s.sem(f"at_neg_in{p}") for p in range(2)]
        v_in, v_split, vh_done = s.sem("at_v_in"), s.sem("at_v_split"), s.sem("at_v_hi")
        ones_done = s.sem("at_ones")
        s_full, e_done, ph_done = s.sem("at_s_full"), s.sem("at_exp"), s.sem("at_ph")
        pl_dve, pl_pool = s.sem("at_pl_dve"), s.sem("at_pl_pool")
        pv_done = s.sem("at_pv")
        mx_full, mx_done = s.sem("at_mx_full"), s.sem("at_mx_done")
        mtop_done, neg_done = s.sem("at_mtop"), s.sem("at_neg")
        o_act = s.sem("at_o_act")
        den_in = [s.sem(f"at_den_in{p}") for p in range(2)]
        rden_done = [s.sem(f"at_rden{p}") for p in range(2)]
        rden_out, rbc_in = s.sem("at_rden_out"), s.sem("at_rbc_in")
        norm_done = s.sem("at_norm")
        hs_out = [s.sem(f"at_hs_out{p}") for p in range(2)]

        STEPS = 2 * KT
        LASTP = G // 2 - 1
        keys = lambda t: P if t < KT - 1 else LASTK

        def wait_low(eng, i, j):
            mine = [k % KT in POOL_T for k in range(STEPS)]
            if mine[j]:
                eng.wait_ge(pl_pool, i * mine.count(True) + mine[:j + 1].count(True))
            else:
                eng.wait_ge(pl_dve, i * mine.count(False) + mine[:j + 1].count(False))

        def make_low(eng, i, j, sem):
            n, r = i * STEPS + j, keys(j % KT)
            eng.wait_ge(ph_done, n + 1)
            eng.tensor_tensor(pl[j % PB][0:r, :], prob[j % PF][0:r, :], ph[j % PB][0:r, :].bitcast(F32),
                              ALU.subtract).then_inc(sem, 1)

        def both(eng, body):
            with eng.Fori(0, LASTP) as i:
                body(i, False)
            body(LASTP, True)

        with nc.Block() as block:
            @block.sync
            def _(sp):
                def load(i, p):
                    r = lambda off, n: bass.ds((2 * i + p) * D + off, n)
                    f = lambda x: x.bitcast(F32)
                    for dst, src, sem in (
                        (f(qa[p][0:D, :]), scratch["qh"][r(0, D), :], qk_in[p]),
                        (f(qa[p][D:P, :]), scratch["qh"][r(0, LO_A), :], qk_in[p]),
                        (f(ka[p][0:D, :]), scratch["kh"][r(0, D), :], qk_in[p]),
                        (f(ka[p][D:P, :]), scratch["kl"][r(0, LO_A), :], qk_in[p]),
                        (f(qb[p][0:D, :]), scratch["ql"][r(0, D), :], qkb_in[p]),
                        (f(qb[p][D:SHIFT, :]), scratch["qh"][r(LO_A, LO_B), :], qkb_in[p]),
                        (f(kb[p][0:D, :]), scratch["kh"][r(0, D), :], qkb_in[p]),
                        (f(kb[p][D:SHIFT, :]), scratch["kl"][r(LO_A, LO_B), :], qkb_in[p]),
                    ):
                        sp.dma_start(dst, src).then_inc(sem, 16)

                def shift(i, p):
                    sp.wait_ge(neg_done, 2 * i + p + 1)
                    sp.dma_start(qb[p][SHIFT:SHIFT + 1, :].rearrange("o (q g) -> o q g", q=P).bitcast(F32),
                                 mneg[:, p, :].bitcast(F32)).then_inc(neg_in[p], 16)

                def finish(i, p):
                    g = 2 * i + p
                    sp.wait_ge(o_act, g + 2)
                    sp.dma_start(den[p][:], o_raw[p][D:DA, :].rearrange("o (p j) -> o p j", p=P)
                                 ).then_inc(den_in[p], 16)
                    sp.wait_ge(rden_done[p], i + 1 + p)
                    sp.dma_start(scratch["rden"][bass.ds(g, 1), :].rearrange("o (p j) -> p (o j)", p=P),
                                 rden[p][:]).then_inc(rden_out, 16)
                    sp.wait_ge(rden_out, (g + 1) * 16)
                    sp.wait_ge(norm_done, g + 1)
                    sp.dma_start(rbc[:, None, :], scratch["rden"][None, bass.ds(g, 1), :].to_broadcast([D, 1, SQ])
                                 ).then_inc(rbc_in, 16)
                    sp.wait_ge(norm_done, g + 2)
                    sp.dma_start(scratch["hs"][bass.ds(g * D, D), :], o_raw[p][0:D, :]).then_inc(hs_out[p], 16)

                def body(i, last):
                    shift(i, 1)
                    if not last:
                        sp.wait_ge(s_full, (2 * i + 1) * KT)
                        load(i + 1, 0)
                    finish(i, 0)
                    if not last:
                        shift(i + 1, 0)
                        sp.wait_ge(s_full, (2 * i + 2) * KT)
                        load(i + 1, 1)
                    finish(i, 1)

                sp.wait_ge(ones_done, 2)
                load(0, 0)
                load(0, 1)
                shift(0, 0)
                both(sp, body)
                for p in range(2):
                    sp.wait_ge(hs_out[p], 16 + 16 * G // 2)

            @block.gpsimd
            def _(pool):
                def split_v(i, p):
                    g = 2 * i + p
                    hi, lo = v_s[p]
                    pool.dma_start(v_f[:], scratch["v"][bass.ds(g, 1), :, :].rearrange("o p n -> p o n")
                                   ).then_inc(v_in, 16)
                    pool.wait_ge(v_in, (g + 1) * 16)
                    src = v_f[:, 0, :].rearrange("p (t d) -> p t d", d=D)
                    pool.tensor_tensor(hi[:, :, 0:D], src, one[:, :, None].to_broadcast([P, KT, D]),
                                       ALU.mult).then_inc(vh_done, 1)
                    pool.wait_ge(vh_done, g + 1)
                    pool.tensor_tensor(lo[:, :, 0:D], src, hi[:, :, 0:D].bitcast(F32),
                                       ALU.subtract).then_inc(v_split, 1)
                    pool.wait_ge(v_split, g + 1)

                def normalise(g, p):
                    pool.wait_ge(rbc_in, g * 16 + 32)
                    pool.tensor_tensor(o_raw[p][0:D, :], o_raw[p][0:D, :], rbc[:], ALU.mult).then_inc(norm_done, 1)
                    pool.wait_ge(norm_done, g + 2)

                def body(i, last):
                    for j in range(STEPS):
                        p, t = divmod(j, KT)
                        if t + 1 in POOL_T:
                            make_low(pool, i, j + 1, pl_pool)
                        if p == 1 and t == 8 and not last:
                            pool.wait_ge(pv_done, PB + (2 * i + 1) * KT)
                            split_v(i + 1, 0)
                        if p == 1 and t == 12:
                            normalise(2 * i, 0)
                        if p == 0 and t == 8:
                            pool.wait_ge(pv_done, PB + 2 * i * KT)
                            split_v(i, 1)
                        if p == 0 and t == 12:
                            normalise(2 * i - 1, 1)

                for p in range(2):
                    pool.memset(kb[p][3 * 32:SHIFT + 1, :].bitcast(F32), 1.0).then_inc(ones_done, 1)
                pool.wait_ge(ones_done, 2)
                for p in range(2):
                    pool.memset(v_s[p][0][:, :, D:DA].bitcast(F32), 1.0).then_inc(ones_done, 1)
                    pool.memset(v_s[p][1][:, :, D:DA].bitcast(F32), 0.0).then_inc(ones_done, 1)
                pool.memset(one[:], 1.0).then_inc(ones_done, 1)
                pool.wait_ge(ones_done, 7)
                pool.memset(rbc[:], 1.0).then_inc(rbc_in, 16)
                pool.wait_ge(rbc_in, 16)
                pool.memset(o_raw[1][0:D, :], 1.0).then_inc(ones_done, 1)
                pool.wait_ge(ones_done, 8)
                split_v(0, 0)
                both(pool, body)
                normalise(G - 1, 1)

            @block.scalar
            def _(act):
                def exp(i, j, before=None, between=lambda: None):
                    n, r = i * STEPS + j, keys(j % KT)
                    act.wait_ge(s_full, n + 1)
                    if j >= PF:
                        wait_low(act, i, j - PF)
                    elif before is not None:
                        wait_low(act, before, j - PF + STEPS)
                    act.activation(prob[j % PF][0:r, :], s_ps[j % 2][0:r, :], ACT.Exp, scale=SCALE
                                   ).then_inc(e_done, 1)
                    between()
                    act.wait_ge(e_done, n + 1)
                    act.wait_ge(pv_done, n + 1)
                    act.activation(ph[j % PB][0:r, :], prob[j % PF][0:r, :], ACT.Copy).then_inc(ph_done, 1)

                def take(i, p):
                    g = 2 * i + p
                    act.wait_ge(pv_done, PB + (g + 1) * KT)
                    act.wait_ge(hs_out[p], (i + 1) * 16)
                    act.activation(o_raw[p][:], o_ps[:], ACT.Copy).then_inc(o_act, 1)

                def body(i, last):
                    for j in range(STEPS):
                        ends = j % KT == KT - 1
                        between = (lambda: take(i, j // KT)) if ends else (lambda: None)
                        if j + 2 < STEPS:
                            exp(i, j + 2, between=between)
                        elif not last:
                            exp(i + 1, j + 2 - STEPS, i, between)
                        else:
                            between()

                act.sem_inc(o_act, 1)
                for p in range(2):
                    act.sem_inc(hs_out[p], 16)
                exp(0, 0)
                exp(0, 1)
                both(act, body)

            @block.vector
            def _(dve):
                def split(i, j):
                    if j % KT not in POOL_T:
                        make_low(dve, i, j, pl_dve)

                def piece(i, p, k):
                    n = (2 * i + p) * MXN + k
                    qt, c = divmod(k, SKV // CH)
                    w = min(CH, SK - c * CH)
                    dve.wait_ge(mx_full, n + 1)
                    dve.tensor_reduce(mpart[:, p, qt, c:c + 1], mx_ps[k % 2][:, 0:w], AX, ALU.max).then_inc(mx_done, 1)

                def top(i, p):
                    g = 2 * i + p
                    dve.wait_ge(mx_done, (g + 1) * MXN)
                    dve.tensor_reduce(mtop[:, p, :], mpart[:, p], AX, ALU.max).then_inc(mtop_done, 1)
                    dve.wait_ge(mtop_done, g + 1)
                    dve.tensor_scalar(mneg[:, p, :], mtop[:, p, :], -1.0, None, ALU.mult).then_inc(neg_done, 1)
                    dve.wait_ge(neg_done, g + 1)

                def invert(p, count):
                    dve.wait_ge(den_in[p], count * 16)
                    dve.reciprocal(rden[p][:], den[p][:]).then_inc(rden_done[p], 1)

                def body(i, last):
                    for j in range(STEPS):
                        p, t = divmod(j, KT)
                        todo = [] if last and p else list(pieces(t))
                        for k in todo[:SPLIT_AT]:
                            piece(i + p, 1 - p, k)
                        if j + 1 < STEPS:
                            split(i, j + 1)
                        elif not last:
                            split(i + 1, 0)
                        for k in todo[SPLIT_AT:]:
                            piece(i + p, 1 - p, k)
                        if todo and todo[-1] == MXN - 1:
                            top(i + p, 1 - p)
                        if j == 3:
                            invert(1, i + 1)
                        if j == KT + 3:
                            invert(0, i + 1)

                dve.memset(den[1][:], 1.0).then_inc(den_in[1], 16)
                for k in range(MXN):
                    piece(0, 0, k)
                top(0, 0)
                split(0, 0)
                both(dve, body)
                invert(1, G // 2 + 1)

            @block.tensor
            def _(pe):
                def piece(i, p, k):
                    n = (2 * i + p) * MXN + k
                    qt, c = divmod(k, SKV // CH)
                    w = min(CH, SK - c * CH)
                    if k == 0:
                        pe.wait_ge(qk_in[p], (i + 1) * 64)
                    if k >= 2 or not isinstance(i, int) or i or p:
                        pe.wait_ge(mx_done, n - 1)
                    pe.matmul(mx_ps[k % 2][:, 0:w], qa[p][:, qt:SQ:ST], ka[p][:, c * CH:c * CH + w],
                              start=True, stop=True).then_inc(mx_full, 1)

                def scores(i, j, between):
                    n = i * STEPS + j
                    p, t = divmod(j, KT)
                    r = keys(t)
                    if t == 0:
                        pe.wait_ge(qk_in[p], (i + 1) * 64)
                        pe.wait_ge(qkb_in[p], (i + 1) * 64)
                        pe.wait_ge(neg_in[p], (i + 1) * 16)
                    if not (isinstance(i, int) and i == 0 and j < 2):
                        pe.wait_ge(e_done, n - 1)
                    for a, y, first in ((ka[p], qa[p], True), (kb[p], qb[p], False)):
                        rows = P if first else SHIFT + 1
                        for u in range(2):
                            mm = pe.matmul(s_ps[j % 2][0:r, u * CH:(u + 1) * CH], a[0:rows, t * P:t * P + r],
                                           y[0:rows, u * CH:(u + 1) * CH], start=first, stop=not first)
                        if first:
                            between()
                    mm.then_inc(s_full, 1)

                def values(i, j, between):
                    n = i * STEPS + j
                    p, t = divmod(j, KT)
                    r = keys(t)
                    if t == 0:
                        pe.wait_ge(v_split, 2 * i + p + 1)
                        pe.wait_ge(o_act, 2 * i + p + 1)
                    wait_low(pe, i, j)
                    hi, lo = v_s[p]
                    for m, (a, y) in enumerate(((hi, ph), (lo, ph), (hi, pl))):
                        for u in range(2):
                            mm = pe.matmul(o_ps[:, u * CH:(u + 1) * CH], a[0:r, t, :],
                                           y[j % PB][0:r, u * CH:(u + 1) * CH],
                                           start=t == 0 and m == 0, stop=t == KT - 1 and m == 2)
                        if m < 2:
                            between()
                    mm.then_inc(pv_done, 1)

                def body(i, last):
                    for j in range(STEPS):
                        p, t = divmod(j, KT)
                        todo = [] if last and p else list(pieces(t))

                        def between():
                            if todo:
                                piece(i + p, 1 - p, todo.pop(0))

                        if j + 2 < STEPS:
                            scores(i, j + 2, between)
                        elif not last:
                            scores(i + 1, j + 2 - STEPS, between)
                        values(i, j, between)
                        assert not todo

                pe.sem_inc(pv_done, PB)
                for k in range(MXN):
                    piece(0, 0, k)
                pe.wait_ge(ones_done, 7)
                for j in range(2):
                    scores(0, j, lambda: None)
                both(pe, body)


def pieces(t):
    assert sum(PIECES) == MXN
    return range(sum(PIECES[:t]), sum(PIECES[:t + 1]))


def output(nc, kept, d, scratch, out):
    with ExitStack() as stack:
        s = Scope(nc, stack)
        wout_f = s.sb("o_wout_f", [P, MC, HID])
        wout = (s.sb("o_wout_hi", [P, MC, HID], F32R), s.sb("o_wout_lo", [P, MC, HID], F32R))
        bias = s.sb("o_bias", [P, HID])
        p2 = s.sb("o_p2", [HT, 1, SQ])
        hs_f = [s.sb(f"o_hs_f{p}", [P, MC, P]) for p in range(2)]
        hs_s = [(s.sb(f"o_hs_hi{p}", [P, MC, P], F32R), s.sb(f"o_hs_lo{p}", [P, MC, P], F32R)) for p in range(2)]
        x_t = [s.sb(f"o_x{p}", [P, HID]) for p in range(2)]
        o_t = [s.sb(f"o_o{p}", [P, HID]) for p in range(2)]
        ps = [s.psum(f"o_ps{p}", [P, 2, CH]) for p in range(2)]

        w_in, w_hi, w_lo, bias_in = s.sem("o_w_in"), s.sem("o_w_hi"), s.sem("o_w_lo"), s.sem("o_bias_in")
        hs_in = [s.sem(f"o_hs_in{p}") for p in range(2)]
        x_in = [s.sem(f"o_x_in{p}") for p in range(2)]
        hi, lo, p2_done = s.sem("o_hi"), s.sem("o_lo"), s.sem("o_p2_done")
        xb, full = s.sem("o_xb"), s.sem("o_full")
        done = s.sem("o_done")
        o_out = [s.sem(f"o_out{p}") for p in range(2)]
        C = 2
        hs_v = scratch["hs"].rearrange("(b m p) q -> b p m q", m=MC, p=P)

        with nc.Block() as block:
            @block.sync
            def _(sp):
                sp.dma_start(wout_f[:], d["wout"].rearrange("(m p) n -> p m n", p=P)).then_inc(w_in, 16)
                sp.dma_start(bias[:], d["bias"].to_broadcast([P, HID])).then_inc(bias_in, 16)
                with sp.Fori(0, B) as b:
                    for t in range(ST):
                        n, p = b * ST + t, t % 2
                        sp.wait_ge(lo, n + 1)
                        sp.dma_start(hs_f[p][:], hs_v[bass.ds(b, 1), :, :, t * P:(t + 1) * P]
                                     .rearrange("o p m q -> p (o m) q")).then_inc(hs_in[p], 16)
                        sp.wait_ge(done, n + 1)
                        sp.dma_start(x_t[p][:], d["x"].rearrange("b s n -> (b s) n")[bass.ds(b * SQ + t * P, P), :]
                                     ).then_inc(x_in[p], 16)

            @block.gpsimd
            def _(pool):
                pool.wait_ge(bias_in, 16)
                with pool.Fori(0, B) as b:
                    for t in range(ST):
                        n, p = b * ST + t, t % 2
                        pool.wait_ge(x_in[p], (b * (ST // 2) + t // 2 + 1) * 16)
                        pool.tensor_tensor(x_t[p][:], x_t[p][:], bias[:], ALU.add).then_inc(xb, 1)

            @block.scalar
            def _(act):
                for p in range(2):
                    act.sem_inc(o_out[p], 16)
                act.wait_ge(w_in, 16)
                act.activation(wout[0][:], wout_f[:], ACT.Copy).then_inc(w_hi, 1)

                def split(b, t):
                    n, p = b * ST + t, t % 2
                    act.wait_ge(hs_in[p], (b * (ST // 2) + t // 2 + 1) * 16)
                    act.wait_ge(full, n + 1)
                    act.activation(hs_s[p][0][:], hs_f[p][:], ACT.Copy).then_inc(hi, 1)

                with act.Fori(0, B) as b:
                    act.wait_ge(full, b * ST + C)
                    act.activation(p2[:], kept["p2g"][:, bass.ds(b, 1), :], ACT.Copy).then_inc(p2_done, 1)
                    split(b, 0)
                    for t in range(ST):
                        if t + 1 < ST:
                            split(b, t + 1)
                        n, p = b * ST + t, t % 2
                        act.wait_ge(done, n + 1 + C)
                        act.dma_start(out[bass.ds(b * SQ + t * P, P), :], o_t[p][:]).then_inc(o_out[p], 16)
                for p in range(2):
                    act.wait_ge(o_out[p], 16 + 16 * B * ST // 2)

            @block.vector
            def _(dve):
                dve.sem_inc(lo, C)
                dve.sem_inc(done, C)
                dve.wait_ge(w_hi, 1)
                dve.tensor_tensor(wout[1][:], wout_f[:], wout[0][:].bitcast(F32), ALU.subtract).then_inc(w_lo, 1)

                def split(b, t):
                    n, p = b * ST + t, t % 2
                    dve.wait_ge(hi, n + 1)
                    dve.tensor_tensor(hs_s[p][1][:], hs_f[p][:], hs_s[p][0][:].bitcast(F32),
                                      ALU.subtract).then_inc(lo, 1)

                with dve.Fori(0, B) as b:
                    split(b, 0)
                    for t in range(ST):
                        if t + 1 < ST:
                            split(b, t + 1)
                        n, p = b * ST + t, t % 2
                        dve.wait_ge(full, n + 1 + C)
                        dve.wait_ge(xb, n + 1)
                        dve.wait_ge(o_out[p], (b * (ST // 2) + t // 2 + 1) * 16)
                        u = lambda a: a.rearrange("p (u n) -> p u n", u=2)
                        dve.tensor_tensor(u(o_t[p][:]), ps[p][:, :, 0:HALF], u(x_t[p][:]), ALU.add).then_inc(done, 1)

            @block.tensor
            def _(pe):
                pe.sem_inc(full, C)
                pe.wait_ge(w_lo, 1)
                with pe.Fori(0, B) as b:
                    pe.wait_ge(p2_done, b + 1)
                    for t in range(ST):
                        n, p = b * ST + t, t % 2
                        pe.wait_ge(lo, n + 1 + C)
                        pe.wait_ge(done, n + 1)
                        for m in range(MC):
                            for i, (a, y) in enumerate(products(hs_s[p], wout)):
                                for u in range(2):
                                    pe.matmul(ps[p][:, u, 0:HALF], a[:, m, :], y[:, m, u * HALF:(u + 1) * HALF],
                                              start=m == 0 and i == 0, stop=False)
                        for u in range(2):
                            mm = pe.matmul(ps[p][:, u, 0:HALF], p2[:, 0, t * P:(t + 1) * P],
                                           kept["vw"][:, bass.ds(b, 1), u * HALF:(u + 1) * HALF], start=False, stop=True)
                        mm.then_inc(full, 1)


def program(nc, d, out):
    dram = lambda name, shape: nc.dram_tensor(name, shape, F32, kind="Internal").ap()
    scratch = {
        "kh": dram("k_hi_d", [B * HID, SKV]), "kl": dram("k_lo_d", [B * HID, SKV]),
        "qh": dram("q_hi_d", [B * HID, SQ]), "ql": dram("q_lo_d", [B * HID, SQ]),
        "v": dram("v_d", [G, P, KT * D]), "hs": dram("heads_d", [B * HID, SQ]), "rden": dram("rden_d", [G, SQ]),
    }
    with ExitStack() as stack:
        s = Scope(nc, stack)
        kept = {
            "u": s.sb("u", [3 * HT + 1, B * SQ], F32R),
            "wk2": s.sb("wk2", [DA, B, NH, HT + 2]),
            "vw": s.sb("vw", [HT, B, HID]),
            "p2g": s.sb("p2g", [HT, B, SQ]),
            "u_ones": s.sem("u_ones"),
        }
        with ExitStack() as inner:
            ws = Scope(nc, inner)
            pair = lambda n, k, c: (ws.sb(f"{n}_hi", [P, k, c], F32R), ws.sb(f"{n}_lo", [P, k, c], F32R))
            w = {"wq": pair("wq", MC, HID), "wk": pair("wk", KC, HID), "wv": pair("wv", KC, HID),
                 "wqca": pair("wqca", MC, 3 * HT)}
            prepare(nc, kept, w, d)
            project(nc, kept, w, d, scratch)
        tokens(nc, kept, d)
        attend(nc, kept, scratch)
        output(nc, kept, d, scratch, out.rearrange("b s n -> (b s) n"))


def layouts(x, ctx, Wq, Wk, Wv, Wq_ca, Wk_ca, Wv_ca, Wout, b_out):
    ca = ctx[:, SK:, :]
    wqca = np.zeros((NH, D, 3, NH, NT), Wq_ca.dtype)
    ca_bd = np.zeros((B, 3, NH, NT, NH, CD), ctx.dtype)
    for h in range(NH):
        for r in range(3):
            wqca[h, :, r, h, :] = Wq_ca[:, h * D:(h + 1) * D].T
            ca_bd[:, r, h, :, h, :] = ca
    mask = np.zeros((NH, D, NH), np.float32)
    for h in range(NH):
        mask[h, :, h] = 1
    frame = np.zeros((DA, B, NH, HT + 2), np.float32)
    frame[D, :, :, HT] = 1
    onehot = np.zeros((P, SQ), np.float32)
    onehot[gather_index() % P, np.arange(SQ)] = 1
    return {
        "x": x, "xT": x.transpose(0, 2, 1), "ctxT": ctx.transpose(0, 2, 1),
        "wq": Wq, "wqT": Wq.T, "wk": Wk, "wv": Wv, "wkca": Wk_ca, "wvca": Wv_ca, "wout": Wout,
        "bias": b_out.reshape(1, HID), "caT": ca.transpose(2, 0, 1).reshape(CD, B * NT),
        "wqca": wqca.reshape(HID, 3 * HT), "caBD": ca_bd.reshape(B, 3 * HT, NH * CD),
        "mask": mask.reshape(HID, NH), "wk2_frame": frame, "onehot": onehot,
    }


def kernel(x, ctx_768, L0_xattn_Wq, L0_xattn_Wk, L0_xattn_Wv, L0_xattn_Wq_ca, L0_xattn_Wk_ca,
           L0_xattn_Wv_ca, L0_xattn_Wout, L0_xattn_b_out):
    import concourse.bacc as bacc
    from concourse.bass_utils import run_bass_kernel_spmd

    a = [np.asarray(v) for v in (x, ctx_768, L0_xattn_Wq, L0_xattn_Wk, L0_xattn_Wv, L0_xattn_Wq_ca,
                                 L0_xattn_Wk_ca, L0_xattn_Wv_ca, L0_xattn_Wout, L0_xattn_b_out)]
    nc = bacc.Bacc("TRN2", target_bir_lowering=False, num_devices=1)
    arrays, d = {}, {}
    for name, v in layouts(*a).items():
        arrays[f"in_{name}"] = np.ascontiguousarray(v)
        d[name] = nc.dram_tensor(f"in_{name}", v.shape, mybir.dt.from_np(v.dtype), kind="ExternalInput").ap()
    out = nc.dram_tensor("out", (B, SQ, HID), F32, kind="ExternalOutput").ap()
    program(nc, d, out)
    r = run_bass_kernel_spmd(nc, [arrays], core_ids=[0])
    return r.results[0]["out"]
```

```python
from contextlib import ExitStack

import concourse.bass as bass
from concourse import mybir
import numpy as np

F32 = mybir.dt.float32
F32R = mybir.dt.float32r
ALU = mybir.AluOpType
ACT = mybir.ActivationFunctionType
AX = mybir.AxisListType.X

P = 128
B, SQ, HID = 2, 1024, 640
SKV, CD, NT = 2048, 384, 4
SK = SKV - NT
NH = 8
D = HID // NH
SCALE = float(D) ** -0.5
MC, KC = HID // P, CD // P
HT = NH * NT
K3 = 3 * HT
CH = 512
HALF = HID // 2
KT = SKV // P
LASTK = SK - (KT - 1) * P
ST = SQ // P
G = B * NH
DA = D + 1
LO_A = P - D
LO_B = D - LO_A
SHIFT = D + LO_B


def gather_index():
    return np.linspace(0, CD - 1, SQ).astype(np.int64)


def products(a, b):
    return ((a[0], b[0]), (a[0], b[1]), (a[1], b[0]))


class Scope:
    def __init__(self, nc, stack):
        self.nc, self.stack = nc, stack

    def sb(self, name, shape, dt=F32):
        return self.stack.enter_context(self.nc.sbuf_tensor(name, shape, dt))

    def psum(self, name, shape, dt=F32):
        return self.stack.enter_context(self.nc.psum_tensor(name, shape, dt))

    def sem(self, name):
        return self.stack.enter_context(self.nc.semaphore(name))


def project(nc, kept, w, d, scratch):
    NS = SKV // CH
    NQ = SQ // CH
    RING = 3
    with ExitStack() as stack:
        s = Scope(nc, stack)
        ctx_f = [s.sb(f"ctx_f{i}", [P, 1, KC, CH]) for i in range(2)]
        ctx_s = [(s.sb(f"ctx_hi{i}", [P, KC, CH], F32R), s.sb(f"ctx_lo{i}", [P, KC, CH], F32R)) for i in range(2)]
        x_f = s.sb("x_f", [P, 1, MC, CH])
        ca_f = s.sb("pj_ca_f", [P, MC * HID])
        ca = kept["ca1"]
        part = s.sb("pj_part", [P, NH * KC, 2])
        top = s.sb("pj_top", [P, NH * KC])
        x_s = (s.sb("x_hi", [P, MC, CH], F32R), s.sb("x_lo", [P, MC, CH], F32R))
        ring = [(s.sb(f"out_hi{i}", [P, CH], F32R), s.sb(f"out_lo{i}", [P, CH], F32R)) for i in range(RING)]
        v_t = s.sb("v_t", [P, 2, NH, CH // P, D])
        banks = [s.psum(f"bank{i}", [P, CH]) for i in range(8)]
        u_all = kept["u"]

        ctx_in = [s.sem(f"pj_ctx_in{i}") for i in range(2)]
        ctx_hi, ctx_lo = s.sem("pj_ctx_hi"), s.sem("pj_ctx_lo")
        x_in, x_hi, x_lo = s.sem("pj_x_in"), s.sem("pj_x_hi"), s.sem("pj_x_lo")
        full, hi_done, done = s.sem("pj_full"), s.sem("pj_hi"), s.sem("pj_done")
        ring_out = [s.sem(f"pj_ring_out{i}") for i in range(RING)]
        v_out = [s.sem(f"pj_v_out{i}") for i in range(2)]

        w_in = [s.sem(f"pj_w_in{n}") for n in range(4)]
        w_hi, w_lo = s.sem("pj_w_hi"), s.sem("pj_w_lo")
        ca_in, ca_hi, ca_lo = s.sem("pj_ca_in"), s.sem("pj_ca_hi"), s.sem("pj_ca_lo")
        top_done = s.sem("pj_top_done")
        flat = v_t[:].rearrange("p a h t d -> p (a h t d)")
        n_k = KC * HID
        stages = [("wk", flat[:, 0:n_k]), ("wv", flat[:, n_k:2 * n_k]),
                  ("wqca", flat[:, 2 * n_k:2 * n_k + MC * K3]), ("wq", ca_f[:])]
        stages = [(n, v.rearrange("p (m n) -> p m n", m=w[n][0].shape[1])) for n, v in stages]

        jobs, maxima = [], [("m", 0, (hc, u)) for hc in range(NH * KC) for u in range(2)]
        for c in range(NS):
            for job in [("k", c, m) for m in range(MC)] + [("v", c, (t, u)) for t in range(4) for u in range(2)]:
                jobs.append(job)
                if c >= NQ:
                    jobs += maxima[:2]
                    maxima = maxima[2:]
            if c < NQ:
                jobs += [("q", c, m) for m in range(MC)] + [("u", c, 0)]
        assert not maxima
        NJ = len(jobs)
        assert NJ % 8 == 0
        split_jobs = [j for j in jobs if j[0] in "kqu"]
        ring_jobs = [j for j in jobs if j[0] in "kq"]
        last = {(kind, c): n for n, (kind, c, _) in enumerate(jobs)}

        def read_ctx(c):
            return last["v", c] + 1 + NJ if c >= 0 else last["v", c + NS] + 1

        def read_x(c):
            return last["u", c] + 1 + NJ if c >= 0 else last["u", c + NQ] + 1

        NSP, NR = len(split_jobs), len(ring_jobs)
        assert NR % RING == 0

        ctxT = d["ctxT"].rearrange("b (m p) s -> p b m s", p=P)
        xT = d["xT"].rearrange("b (m p) s -> p b m s", p=P)

        with nc.Block() as block:
            @block.gpsimd
            def _(pool):
                pool.sem_inc(ctx_lo, 2)
                pool.sem_inc(x_lo, 1)
                pool.sem_inc(ca_lo, 1)
                pool.memset(u_all[K3:K3 + 1, :].bitcast(F32), 1.0).then_inc(kept["u_ones"], 1)
                with pool.Fori(0, B) as b:
                    for c in range(NS):
                        pool.wait_ge(ctx_lo, b * NS + c + 1)
                        pool.dma_start(ctx_f[c % 2][:], ctxT[:, bass.ds(b, 1), :, c * CH:(c + 1) * CH]
                                       ).then_inc(ctx_in[c % 2], 16)
                        if c < NQ:
                            q = c
                            pool.wait_ge(x_lo, b * NQ + q + 1)
                            pool.dma_start(x_f[:], xT[:, bass.ds(b, 1), :, q * CH:(q + 1) * CH]
                                           ).then_inc(x_in, 16)
                        if c == 1:
                            pool.wait_ge(w_lo, len(stages))
                            pool.wait_ge(ca_lo, b + 1)
                            pool.dma_start(ca_f[0:K3, None, 0:NH * CD], d["caBD"].rearrange("b k n -> k b n")
                                           [:, bass.ds(b, 1), :]).then_inc(ca_in, 16)

            @block.sync
            def _(sp):
                for n, (name, stage) in enumerate(stages):
                    sp.dma_start(stage, d[name].rearrange("(m p) n -> p m n", p=P)).then_inc(w_in[n], 16)
                with sp.Fori(0, B) as b:
                    nr = ns = 0
                    for n, (kind, c, m) in enumerate(jobs):
                        if kind in "kq":
                            hi, lo = ring[nr % RING]
                            to = scratch["kh"], scratch["kl"]
                            if kind == "q":
                                to = scratch["qh"], scratch["ql"]
                            at = (bass.ds(b * HID + m * P, P), slice(c * CH, (c + 1) * CH))
                            sp.wait_ge(hi_done, b * NSP + ns + 1)
                            sp.dma_start(to[0][at], hi[:].bitcast(F32)).then_inc(ring_out[nr % RING], 16)
                            sp.wait_ge(done, b * NJ + n + 1 + 8)
                            sp.dma_start(to[1][at], lo[:].bitcast(F32)).then_inc(ring_out[nr % RING], 16)
                            nr += 1
                        if kind in "kqu":
                            ns += 1
                        if kind == "v" and m == (3, 1):
                            sp.wait_ge(done, b * NJ + n + 1 + 8)
                            sp.dma_start(scratch["v"][bass.ds(b * NH, NH), :, c * 4 * D:(c + 1) * 4 * D]
                                         .rearrange("h p n -> p h n"),
                                         v_t[:, c % 2].rearrange("p h t d -> p h (t d)")).then_inc(v_out[c % 2], 16)
                for i in range(RING):
                    sp.wait_ge(ring_out[i], 32 + B * NR // RING * 32)
                for i in range(2):
                    sp.wait_ge(v_out[i], 16 + B * NS // 2 * 16)

            @block.scalar
            def _(act):
                for i in range(RING):
                    act.sem_inc(ring_out[i], 32)

                def split_ctx(b, c):
                    act.wait_ge(ctx_in[c % 2], (b * (NS // 2) + c // 2 + 1) * 16)
                    act.wait_ge(full, b * NJ + read_ctx(c - 2))
                    act.activation(ctx_s[c % 2][0][:], ctx_f[c % 2][:, 0], ACT.Copy).then_inc(ctx_hi, 1)

                def split_x(b, q):
                    act.wait_ge(x_in, (b * NQ + q + 1) * 16)
                    act.wait_ge(full, b * NJ + read_x(q - 1))
                    act.activation(x_s[0][:], x_f[:, 0], ACT.Copy).then_inc(x_hi, 1)

                def split_ca(b):
                    act.wait_ge(ca_in, (b + 1) * 16)
                    act.wait_ge(full, b * NJ + NJ)
                    act.activation(ca[0:K3, :], ca_f[0:K3, 0:NH * CD], ACT.Copy).then_inc(ca_hi, 1)

                for n, (name, stage) in enumerate(stages):
                    act.wait_ge(w_in[n], 16)
                    act.activation(w[name][0][:], stage, ACT.Copy).then_inc(w_hi, 1)
                with act.Fori(0, B) as b:
                    nr = 0
                    split_ctx(b, 0)
                    split_x(b, 0)
                    for n, (kind, c, m) in enumerate(jobs):
                        if kind == "k" and m == 0 and c < NS - 1:
                            split_ctx(b, c + 1)
                        if kind == "k" and m == 0 and c == 1:
                            split_x(b, 1)
                        if kind == "q" and m == 0 and c == 1:
                            split_ca(b)
                        if kind in "vm":
                            continue
                        act.wait_ge(full, b * NJ + n + 1 + NJ)
                        if kind == "u":
                            dst = u_all[0:K3, bass.ds(b * SQ + c * CH, CH)]
                            act.activation(dst, banks[n % 8][0:K3, :], ACT.Copy).then_inc(hi_done, 1)
                        else:
                            act.wait_ge(ring_out[nr % RING], (b * (NR // RING) + nr // RING + 1) * 32)
                            act.activation(ring[nr % RING][0][:], banks[n % 8][:], ACT.Copy).then_inc(hi_done, 1)
                            nr += 1

            @block.vector
            def _(dve):
                for i in range(2):
                    dve.sem_inc(v_out[i], 16)

                def split_ctx(b, c):
                    dve.wait_ge(ctx_hi, b * NS + c + 1)
                    hi, lo = ctx_s[c % 2]
                    dve.tensor_tensor(lo[:], ctx_f[c % 2][:, 0], hi[:].bitcast(F32), ALU.subtract).then_inc(ctx_lo, 1)

                def split_x(b, q):
                    dve.wait_ge(x_hi, b * NQ + q + 1)
                    hi, lo = x_s
                    dve.tensor_tensor(lo[:], x_f[:, 0], hi[:].bitcast(F32), ALU.subtract).then_inc(x_lo, 1)

                def split_ca(b):
                    dve.wait_ge(ca_hi, b + 1)
                    rows = slice(HT, 2 * HT)
                    dve.tensor_tensor(ca[rows, :], ca_f[rows, 0:NH * CD], ca[rows, :].bitcast(F32),
                                      ALU.subtract).then_inc(ca_lo, 1)

                for n, (name, stage) in enumerate(stages):
                    dve.wait_ge(w_hi, n + 1)
                    dve.tensor_tensor(w[name][1][:], stage, w[name][0][:].bitcast(F32),
                                      ALU.subtract).then_inc(w_lo, 1)
                dve.wait_ge(w_lo, len(stages))
                with dve.Fori(0, B) as b:
                    nr = ns = 0
                    split_ctx(b, 0)
                    split_x(b, 0)
                    for n, (kind, c, m) in enumerate(jobs):
                        if kind == "k" and m == 0 and c < NS - 1:
                            split_ctx(b, c + 1)
                        if kind == "k" and m == 0 and c == 1:
                            split_x(b, 1)
                        if kind == "q" and m == 0 and c == 1:
                            split_ca(b)
                        bank = banks[n % 8]
                        if kind == "m":
                            hc, u = m
                            dve.wait_ge(full, b * NJ + n + 1 + NJ)
                            dve.tensor_reduce(part[:, hc, u:u + 1], bank[:], AX, ALU.max).then_inc(done, 1)
                            continue
                        if kind == "v":
                            t, u = m
                            dve.wait_ge(full, b * NJ + n + 1 + NJ)
                            if t == 0 and u == 0:
                                dve.wait_ge(v_out[c % 2], (b * (NS // 2) + c // 2 + 1) * 16)
                            dve.tensor_copy(v_t[:, c % 2, u * 4:(u + 1) * 4, t, :],
                                            bank[:, 0:HALF].rearrange("p (h d) -> p h d", d=D)).then_inc(done, 1)
                            continue
                        dve.wait_ge(hi_done, b * NSP + ns + 1)
                        if kind == "u":
                            dst = u_all[2 * HT:K3, bass.ds(b * SQ + c * CH, CH)]
                            dve.tensor_tensor(dst, bank[2 * HT:K3, :], dst.bitcast(F32),
                                              ALU.subtract).then_inc(done, 1)
                        else:
                            hi, lo = ring[nr % RING]
                            dve.tensor_tensor(lo[:], bank[:], hi[:].bitcast(F32), ALU.subtract).then_inc(done, 1)
                            nr += 1
                        ns += 1
                    dve.wait_ge(done, b * NJ + NJ + 8)
                    dve.tensor_reduce(top[:], part[:], AX, ALU.max).then_inc(top_done, 1)
                    dve.wait_ge(top_done, b * 2 + 1)
                    dve.tensor_scalar(kept["ntop"][:, bass.ds(b, 1), :], top[:, None, :], -1.0, None,
                                      ALU.mult).then_inc(top_done, 1)
                    dve.wait_ge(top_done, b * 2 + 2)

            @block.tensor
            def _(pe):
                pe.wait_ge(w_lo, len(stages))
                pe.sem_inc(done, 8)
                pe.sem_inc(full, NJ)
                with pe.Fori(0, B) as b:
                    for n, (kind, c, m) in enumerate(jobs):
                        bank = banks[n % 8]
                        if kind == "k" and m == 0:
                            pe.wait_ge(ctx_lo, b * NS + c + 1 + 2)
                        if kind == "q" and m == 0:
                            pe.wait_ge(x_lo, b * NQ + c + 1 + 1)
                        pe.wait_ge(done, b * NJ + n + 1)
                        if kind == "m":
                            hc, u = m
                            if (hc, u) == (0, 0):
                                pe.wait_ge(ca_lo, b + 2)
                                pe.wait_ge(done, b * NJ + last["u", NQ - 1] + 1 + 8)
                            at = hc // KC * CD + hc % KC
                            pe.matmul(bank[:], ca[0:K3, at:at + (P - 1) * KC + 1:KC],
                                      u_all[0:K3, bass.ds(b * SQ + u * CH, CH)], start=True, stop=True
                                      ).then_inc(full, 1)
                            continue
                        nk = {"k": KC, "v": KC, "q": MC, "u": MC}[kind]
                        mm = None
                        for k in range(nk):
                            if kind == "k":
                                pairs = [(a[:, k, m * P:(m + 1) * P], y[:, k, :])
                                         for a, y in products(w["wk"], ctx_s[c % 2])]
                                to = bank[:]
                            elif kind == "v":
                                t, u = m
                                pairs = [(a[:, k, t * P:(t + 1) * P], y[:, k, u * HALF:(u + 1) * HALF])
                                         for a, y in products(ctx_s[c % 2], w["wv"])]
                                to = bank[:, 0:HALF]
                            elif kind == "q":
                                pairs = [(a[:, k, m * P:(m + 1) * P], y[:, k, :]) for a, y in products(w["wq"], x_s)]
                                to = bank[:]
                            else:
                                pairs = [(a[:, k, :], y[:, k, :]) for a, y in products(w["wqca"], x_s)]
                                to = bank[0:K3, :]
                            for i, (a, y) in enumerate(pairs):
                                mm = pe.matmul(to, a, y, start=k == 0 and i == 0, stop=k == nk - 1 and i == 2)
                        mm.then_inc(full, 1)


def tokens(nc, kept, d):
    with ExitStack() as stack:
        s = Scope(nc, stack)
        wqT = s.sb("wqT", [P, MC, HID])
        wout = s.sb("wout_f", [P, MC, HID])
        wkca = s.sb("wkca", [P, KC, HID])
        wvca = s.sb("wvca", [P, KC, HID])
        caT = s.sb("caT", [P, KC, B * NT])
        mask = s.sb("mask", [P, MC, NH])
        tok = [s.sb(f"tok{i}", [P, MC, B * NT]) for i in range(2)]
        bd = [s.sb(f"bd{i}", [P, MC, B, NH, NT]) for i in range(2)]
        ca_f = s.sb("ca_f", [P, NH * CD])
        ca = [s.sb("ca0", [P, NH * CD], F32R), kept["ca1"]]
        xn = [s.sb(f"xn{b}", [P, ST, NH, DA]) for b in range(B)]
        onehot = s.sb("onehot", [P, SQ])
        p1 = [s.sb(f"p1_{i}", [P, 2, CD]) for i in range(3)]
        raw = [s.sb(f"raw{i}", [DA, CD]) for i in range(2)]
        rden = s.sb("tk_rden", [P, 2, KC])
        s2 = s.sb("s2", [P, B, KC, HT])
        t2 = s.sb("t2", [P, B, KC * NH])
        r2 = s.sb("r2", [P, B, KC * NH])
        p2 = s.sb("p2", [P, B, KC, HT])
        f_ps = [s.psum(f"f_ps{i}", [P, CH]) for i in range(2)]
        s_ps = [s.psum(f"s_ps{i}", [P, 2, CH]) for i in range(2)]
        acc_ps = s.psum("acc_ps", [DA, CH])
        t_ps = s.psum("t_ps", [P, KC, HT + 2])

        small_in, wqT_in, wout_in = s.sem("tk_small_in"), s.sem("tk_wqT_in"), s.sem("tk_wout_in")
        tok_full, tok_done, bd_done = s.sem("tk_tok_full"), s.sem("tk_tok"), s.sem("tk_bd")
        wk2_in, wk2_full, wk2_done = s.sem("tk_wk2_in"), s.sem("tk_wk2_full"), s.sem("tk_wk2")
        vw_full, vw_done = s.sem("tk_vw_full"), s.sem("tk_vw")
        ca_in, ca_hi, ca_lo = s.sem("tk_ca_in"), s.sem("tk_ca_hi"), s.sem("tk_ca_lo")
        pairs = ST // 2
        xn_in = [[s.sem(f"tk_xn_in{b}_{j}") for j in range(pairs)] for b in range(B)]
        oh_in = s.sem("tk_onehot_in")
        xn_ones = s.sem("tk_xn_ones")
        ntop_in = [s.sem(f"tk_ntop_in{b}") for b in range(B)]
        s_full, e_done, pv_done = s.sem("tk_s_full"), s.sem("tk_exp"), s.sem("tk_pv")
        raw_done, t_full = s.sem("tk_raw"), s.sem("tk_t_full")
        step = s.sem("tk_step")
        d2_done, e2_done, p2_done = s.sem("tk_d2"), s.sem("tk_e2"), s.sem("tk_p2")
        g_full, g_done = s.sem("tk_g_full"), s.sem("tk_g_done")

        idx = gather_index()
        spans = []
        for c in range(KC):
            q = np.flatnonzero(idx // P == c)
            lo, hi = int(q[0]), int(q[-1]) + 1
            cuts = [lo, CH, hi] if lo < CH < hi else [lo, hi]
            spans += [(c, a, z) for a, z in zip(cuts, cuts[1:])]
        order = (1, 0)
        heads = [(b, h) for b in order for h in range(NH)]
        rows = lambda a: a.rearrange("(m p) n -> p m n", p=P)

        with nc.Block() as block:
            @block.sync
            def _(sp):
                xv = d["x"].rearrange("b (t p) (h d) -> b p t h d", p=P, d=D)

                def shift(b):
                    for h in range(NH):
                        row = ca[b][K3:K3 + 1, h * CD:(h + 1) * CD].rearrange("o (p c) -> o p c", c=KC)
                        sp.dma_start(row.bitcast(F32), kept["ntop"][:, b, h * KC:(h + 1) * KC].bitcast(F32)
                                     ).then_inc(ntop_in[b], 16)

                def values(b):
                    for t in range(ST):
                        sp.dma_start(xn[b][:, t, :, 0:D], xv[b, :, t]).then_inc(xn_in[b][t // 2], 16)

                shift(1)
                values(1)
                sp.dma_start(wkca[:], rows(d["wkca"])).then_inc(small_in, 16)
                sp.dma_start(caT[:], rows(d["caT"])).then_inc(small_in, 16)
                sp.dma_start(mask[:], rows(d["mask"])).then_inc(small_in, 16)
                sp.dma_start(wvca[:], rows(d["wvca"])).then_inc(small_in, 16)
                sp.dma_start(kept["wk2"][:], d["wk2_frame"]).then_inc(wk2_in, 16)
                sp.dma_start(wqT[:], rows(d["wqT"])).then_inc(wqT_in, 16)
                sp.dma_start(ca_f[0:K3, :], d["caBD"][0]).then_inc(ca_in, 16)
                shift(0)
                sp.dma_start(wout[:], rows(d["wout"])).then_inc(wout_in, 16)
                values(0)
                sp.dma_start(onehot[:], d["onehot"]).then_inc(oh_in, 16)

            @block.gpsimd
            def _(pool):
                for b in order:
                    pool.memset(xn[b][:, :, :, D:DA], 1.0).then_inc(xn_ones, 1)

            @block.scalar
            def _(act):
                def raw_out(n):
                    act.wait_ge(pv_done, (n + 1) * pairs)
                    if n >= 2:
                        act.wait_ge(t_full, n - 1)
                    act.activation(raw[n % 2][:], acc_ps[:, 0:CD], ACT.Copy).then_inc(raw_done, 1)

                for n, (b, h) in enumerate(heads):
                    for j in range(pairs):
                        k = n * pairs + j
                        act.wait_ge(s_full, k + 1)
                        if k >= 3:
                            act.wait_ge(pv_done, k - 2)
                        act.activation(p1[k % 3][:], s_ps[k % 2][:, :, 0:CD], ACT.Exp,
                                       scale=SCALE).then_inc(e_done, 1)
                        if j == 1 and n:
                            raw_out(n - 1)
                    if n == 3:
                        act.wait_ge(ca_in, 16)
                        act.activation(ca[0][0:K3, :], ca_f[0:K3, :], ACT.Copy).then_inc(ca_hi, 1)
                    if n in VW_AT:
                        i = VW_AT.index(n)
                        act.wait_ge(vw_full, i + 1)
                        for u in range(2):
                            act.activation(kept["vw"][:, i, u * HALF:(u + 1) * HALF], f_ps[u][0:HT, 0:HALF],
                                           ACT.Copy).then_inc(vw_done, 1)
                raw_out(len(heads) - 1)
                for i, b in enumerate(order):
                    act.wait_ge(d2_done, i + 1)
                    act.activation(s2[:, b], s2[:, b], ACT.Exp, scale=SCALE).then_inc(e2_done, 1)

            @block.vector
            def _(dve):
                steps = [0]

                def chained(ins):
                    steps[0] += 1
                    ins.then_inc(step, 1)
                    dve.wait_ge(step, steps[0])

                def fold(n):
                    b, h = heads[n]
                    dve.wait_ge(t_full, n + 1)
                    chained(dve.reciprocal(rden[:, n % 2, :], t_ps[:, :, HT]))
                    for c in range(KC):
                        r = rden[:, n % 2, c:c + 1]
                        if h == 0:
                            chained(dve.tensor_scalar(s2[:, b, c, :], t_ps[:, c, 0:HT], r, None, ALU.mult))
                        else:
                            chained(dve.scalar_tensor_tensor(out=s2[:, b, c, :], in0=t_ps[:, c, 0:HT], scalar=r,
                                                             in1=s2[:, b, c, :], op0=ALU.mult, op1=ALU.add))

                def center(b):
                    v = s2[:, b].rearrange("p c (h t) -> p (c h) t", t=NT)
                    chained(dve.tensor_reduce(t2[:, b, :], v, AX, ALU.max))
                    dve.tensor_tensor(v, v, t2[:, b, :, None].to_broadcast([P, KC * NH, NT]),
                                      ALU.subtract).then_inc(d2_done, 1)

                def weigh(i, b):
                    v = s2[:, b].rearrange("p c (h t) -> p (c h) t", t=NT)
                    dve.wait_ge(e2_done, i + 1)
                    chained(dve.tensor_reduce(t2[:, b, :], v, AX, ALU.add))
                    chained(dve.reciprocal(r2[:, b, :], t2[:, b, :]))
                    dve.tensor_tensor(p2[:, b].rearrange("p c (h t) -> p (c h) t", t=NT), v,
                                      r2[:, b, :, None].to_broadcast([P, KC * NH, NT]), ALU.mult).then_inc(p2_done, 1)

                for i in range(2):
                    dve.wait_ge(tok_full, i + 1)
                    dve.tensor_copy(tok[i][:], f_ps[i][:, 0:MC * B * NT].rearrange("p (m t) -> p m t", m=MC)
                                    ).then_inc(tok_done, 1)
                dve.wait_ge(small_in, 64)
                dve.wait_ge(tok_done, 2)
                for i in range(2):
                    for b in range(B):
                        t = tok[i][:, :, None, b * NT:(b + 1) * NT].to_broadcast([P, MC, NH, NT])
                        own = mask[:, :, :, None].to_broadcast([P, MC, NH, NT])
                        dve.tensor_tensor(bd[i][:, :, b], t, own, ALU.mult).then_inc(bd_done, 1)
                dve.wait_ge(wk2_full, 1)
                dve.wait_ge(wk2_in, 16)
                for b in range(B):
                    dve.tensor_copy(kept["wk2"][0:D, b, :, 0:HT],
                                    f_ps[0][0:D, :].rearrange("p (h b n) -> p b h n", h=NH, b=B)[:, b]
                                    ).then_inc(wk2_done, 1)
                for n in range(len(heads)):
                    if n == 4:
                        dve.wait_ge(ca_hi, 1)
                        r = slice(HT, 2 * HT)
                        dve.tensor_tensor(ca[0][r, :], ca_f[r, :], ca[0][r, :].bitcast(F32),
                                          ALU.subtract).then_inc(ca_lo, 1)
                    fold(n)
                for b in order:
                    center(b)
                for i, b in enumerate(order):
                    weigh(i, b)
                for i, b in enumerate(order):
                    dve.wait_ge(g_full, i + 1)
                    dve.tensor_copy(kept["p2g"][:, b, :], s_ps[b][0:HT].rearrange("p u n -> p (u n)")
                                    ).then_inc(g_done, 1)
                dve.wait_ge(g_done, B)

            @block.tensor
            def _(pe):
                def fold_tokens():
                    pe.wait_ge(small_in, 64)
                    for i, wt in enumerate((wkca, wvca)):
                        for m in range(MC):
                            for c in range(KC):
                                mm = pe.matmul(f_ps[i][:, m * B * NT:(m + 1) * B * NT], wt[:, c, m * P:(m + 1) * P],
                                               caT[:, c, :], start=c == 0, stop=c == KC - 1)
                        mm.then_inc(tok_full, 1)

                def fold_keys():
                    pe.wait_ge(wqT_in, 16)
                    pe.wait_ge(bd_done, 2 * B)
                    for h in range(NH):
                        for m in range(MC):
                            mm = pe.matmul(f_ps[0][0:D, h * B * HT:(h + 1) * B * HT], wqT[:, m, h * D:(h + 1) * D],
                                           bd[0][:, m].rearrange("p b h t -> p (b h t)"),
                                           start=m == 0, stop=m == MC - 1)
                    mm.then_inc(wk2_full, 1)

                def fold_values(b):
                    pe.wait_ge(wout_in, 16)
                    if b:
                        pe.wait_ge(vw_done, 2 * b)
                    for u in range(2):
                        for m in range(MC):
                            mm = pe.matmul(f_ps[u][0:HT, 0:HALF], bd[1][:, m, b].rearrange("p h t -> p (h t)"),
                                           wout[:, m, u * HALF:(u + 1) * HALF], start=m == 0, stop=m == MC - 1)
                    mm.then_inc(vw_full, 1)

                def scores(k):
                    n, j = divmod(k, pairs)
                    b, h = heads[n]
                    if k % (NH * pairs) == 0:
                        pe.wait_ge(ntop_in[b], 16 * NH)
                        if b == 0:
                            pe.wait_ge(ca_lo, 1)
                    if k >= 2:
                        pe.wait_ge(e_done, k - 1)
                    for t in range(2):
                        st = 2 * j + t
                        mm = pe.matmul(s_ps[k % 2][:, t, 0:CD],
                                       kept["u"][0:K3 + 1, b * SQ + st * P:b * SQ + (st + 1) * P],
                                       ca[b][0:K3 + 1, h * CD:(h + 1) * CD], start=True, stop=True)
                    mm.then_inc(s_full, 1)

                def token_scores(n):
                    b, h = heads[n]
                    if n == 0:
                        pe.wait_ge(wk2_done, B)
                    pe.wait_ge(raw_done, n + 1)
                    if n:
                        pe.wait_ge(step, 4 * n)
                    for c in range(KC):
                        mm = pe.matmul(t_ps[:, c, :], raw[n % 2][:, c * P:(c + 1) * P],
                                       kept["wk2"][:, b, h, :], start=True, stop=True)
                    mm.then_inc(t_full, 1)

                pe.wait_ge(kept["u_ones"], 1)
                pe.wait_ge(xn_ones, B)
                total = len(heads) * pairs
                scores(0)
                for k in range(total):
                    n, j = divmod(k, pairs)
                    b, h = heads[n]
                    if k + 1 < total:
                        scores(k + 1)
                    if n == 0 or (b == 0 and h == 0):
                        pe.wait_ge(xn_in[b][j], 32)
                    pe.wait_ge(e_done, k + 1)
                    if j == 0 and n:
                        pe.wait_ge(raw_done, n)
                    for t in range(2):
                        mm = pe.matmul(acc_ps[:, 0:CD], xn[b][:, 2 * j + t, h, :], p1[k % 3][:, t, :],
                                       start=j == 0 and t == 0, stop=j == pairs - 1 and t == 1)
                    mm.then_inc(pv_done, 1)
                    if k == 3:
                        fold_tokens()
                    if k == 5:
                        fold_keys()
                    if j == 1 and n:
                        token_scores(n - 1)
                    if j == 0 and n in VW_AT:
                        i = VW_AT.index(n)
                        if i == 0:
                            pe.wait_ge(wk2_done, B)
                        fold_values(i)
                token_scores(len(heads) - 1)
                pe.wait_ge(oh_in, 16)
                for i, b in enumerate(order):
                    pe.wait_ge(p2_done, i + 1)
                    for c, a, z in spans:
                        mm = pe.matmul(s_ps[b][0:HT, a // CH, a % CH:a % CH + z - a], p2[:, b, c, :],
                                       onehot[:, a:z], start=True, stop=True)
                    mm.then_inc(g_full, 1)


VW_AT = (5, 6)


PB = 4
PF = 2
MXN = ST * SKV // CH
PIECES = (2, 3, 2, 3, 3, 2, 3, 3, 2, 3, 3, 3)
POOL_T = ()
SPLIT_AT = 1


def attend(nc, kept, scratch):
    with ExitStack() as stack:
        s = Scope(nc, stack)
        ka = [s.sb(f"ka{p}", [P, SKV], F32R) for p in range(2)]
        kb = [s.sb(f"kb{p}", [P, SKV], F32R) for p in range(2)]
        qa = [s.sb(f"qa{p}", [P, SQ], F32R) for p in range(2)]
        qb = [s.sb(f"qb{p}", [P, SQ], F32R) for p in range(2)]
        v_f = s.sb("v_f", [P, 1, KT * D])
        v_s = [(s.sb(f"v_hi{p}", [P, KT, DA], F32R), s.sb(f"v_lo{p}", [P, KT, DA], F32R)) for p in range(2)]
        prob = [s.sb(f"prob{i}", [P, SQ]) for i in range(PF)]
        ph = [s.sb(f"prob_hi{i}", [P, SQ], F32R) for i in range(PB)]
        pl = [s.sb(f"prob_lo{i}", [P, SQ], F32R) for i in range(PB)]
        mpart = s.sb("mpart", [P, 2, ST, SKV // CH])
        mtop = s.sb("mtop", [P, 2, ST])
        mneg = s.sb("mneg", [P, 2, ST], F32R)
        o_raw = [s.sb(f"o_raw{p}", [DA, SQ]) for p in range(2)]
        den = [s.sb(f"den{p}", [P, ST]) for p in range(2)]
        rden = [s.sb(f"rden{p}", [P, ST]) for p in range(2)]
        rbc = s.sb("rbc", [D, SQ])
        one = s.sb("one", [P, 1])
        s_ps = [s.psum(f"at_s_ps{i}", [P, SQ]) for i in range(2)]
        o_ps = s.psum("at_o_ps", [DA, SQ])
        mx_ps = [s.psum(f"at_mx_ps{i}", [P, CH]) for i in range(2)]

        qk_in = [s.sem(f"at_qk_in{p}") for p in range(2)]
        qkb_in = [s.sem(f"at_qkb_in{p}") for p in range(2)]
        neg_in = [s.sem(f"at_neg_in{p}") for p in range(2)]
        v_in, v_split, vh_done = s.sem("at_v_in"), s.sem("at_v_split"), s.sem("at_v_hi")
        ones_done = s.sem("at_ones")
        s_full, e_done, ph_done = s.sem("at_s_full"), s.sem("at_exp"), s.sem("at_ph")
        pl_dve, pl_pool = s.sem("at_pl_dve"), s.sem("at_pl_pool")
        pv_done = s.sem("at_pv")
        mx_full, mx_done = s.sem("at_mx_full"), s.sem("at_mx_done")
        mtop_done, neg_done = s.sem("at_mtop"), s.sem("at_neg")
        o_act = s.sem("at_o_act")
        den_in = [s.sem(f"at_den_in{p}") for p in range(2)]
        rden_done = [s.sem(f"at_rden{p}") for p in range(2)]
        rden_out, rbc_in = s.sem("at_rden_out"), s.sem("at_rbc_in")
        norm_done = s.sem("at_norm")
        hs_out = [s.sem(f"at_hs_out{p}") for p in range(2)]

        STEPS = 2 * KT
        LASTP = G // 2 - 1
        keys = lambda t: P if t < KT - 1 else LASTK

        def wait_low(eng, i, j):
            mine = [k % KT in POOL_T for k in range(STEPS)]
            if mine[j]:
                eng.wait_ge(pl_pool, i * mine.count(True) + mine[:j + 1].count(True))
            else:
                eng.wait_ge(pl_dve, i * mine.count(False) + mine[:j + 1].count(False))

        def make_low(eng, i, j, sem):
            n, r = i * STEPS + j, keys(j % KT)
            eng.wait_ge(ph_done, n + 1)
            eng.tensor_tensor(pl[j % PB][0:r, :], prob[j % PF][0:r, :], ph[j % PB][0:r, :].bitcast(F32),
                              ALU.subtract).then_inc(sem, 1)

        def both(eng, body):
            with eng.Fori(0, LASTP) as i:
                body(i, False)
            body(LASTP, True)

        with nc.Block() as block:
            @block.sync
            def _(sp):
                def load(i, p):
                    r = lambda off, n: bass.ds((2 * i + p) * D + off, n)
                    f = lambda x: x.bitcast(F32)
                    for dst, src, sem in (
                        (f(qa[p][0:D, :]), scratch["qh"][r(0, D), :], qk_in[p]),
                        (f(qa[p][D:P, :]), scratch["qh"][r(0, LO_A), :], qk_in[p]),
                        (f(ka[p][0:D, :]), scratch["kh"][r(0, D), :], qk_in[p]),
                        (f(ka[p][D:P, :]), scratch["kl"][r(0, LO_A), :], qk_in[p]),
                        (f(qb[p][0:D, :]), scratch["ql"][r(0, D), :], qkb_in[p]),
                        (f(qb[p][D:SHIFT, :]), scratch["qh"][r(LO_A, LO_B), :], qkb_in[p]),
                        (f(kb[p][0:D, :]), scratch["kh"][r(0, D), :], qkb_in[p]),
                        (f(kb[p][D:SHIFT, :]), scratch["kl"][r(LO_A, LO_B), :], qkb_in[p]),
                    ):
                        sp.dma_start(dst, src).then_inc(sem, 16)

                def shift(i, p):
                    sp.wait_ge(neg_done, 2 * i + p + 1)
                    sp.dma_start(qb[p][SHIFT:SHIFT + 1, :].rearrange("o (q g) -> o q g", q=P).bitcast(F32),
                                 mneg[:, p, :].bitcast(F32)).then_inc(neg_in[p], 16)

                def finish(i, p):
                    g = 2 * i + p
                    sp.wait_ge(o_act, g + 2)
                    sp.dma_start(den[p][:], o_raw[p][D:DA, :].rearrange("o (p j) -> o p j", p=P)
                                 ).then_inc(den_in[p], 16)
                    sp.wait_ge(rden_done[p], i + 1 + p)
                    sp.dma_start(scratch["rden"][bass.ds(g, 1), :].rearrange("o (p j) -> p (o j)", p=P),
                                 rden[p][:]).then_inc(rden_out, 16)
                    sp.wait_ge(rden_out, (g + 1) * 16)
                    sp.wait_ge(norm_done, g + 1)
                    sp.dma_start(rbc[:, None, :], scratch["rden"][None, bass.ds(g, 1), :].to_broadcast([D, 1, SQ])
                                 ).then_inc(rbc_in, 16)
                    sp.wait_ge(norm_done, g + 2)
                    sp.dma_start(scratch["hs"][bass.ds(g * D, D), :], o_raw[p][0:D, :]).then_inc(hs_out[p], 16)

                def body(i, last):
                    shift(i, 1)
                    if not last:
                        sp.wait_ge(s_full, (2 * i + 1) * KT)
                        load(i + 1, 0)
                    finish(i, 0)
                    if not last:
                        shift(i + 1, 0)
                        sp.wait_ge(s_full, (2 * i + 2) * KT)
                        load(i + 1, 1)
                    finish(i, 1)

                sp.wait_ge(ones_done, 2)
                load(0, 0)
                load(0, 1)
                shift(0, 0)
                both(sp, body)
                for p in range(2):
                    sp.wait_ge(hs_out[p], 16 + 16 * G // 2)

            @block.gpsimd
            def _(pool):
                def split_v(i, p):
                    g = 2 * i + p
                    hi, lo = v_s[p]
                    pool.dma_start(v_f[:], scratch["v"][bass.ds(g, 1), :, :].rearrange("o p n -> p o n")
                                   ).then_inc(v_in, 16)
                    pool.wait_ge(v_in, (g + 1) * 16)
                    src = v_f[:, 0, :].rearrange("p (t d) -> p t d", d=D)
                    pool.tensor_tensor(hi[:, :, 0:D], src, one[:, :, None].to_broadcast([P, KT, D]),
                                       ALU.mult).then_inc(vh_done, 1)
                    pool.wait_ge(vh_done, g + 1)
                    pool.tensor_tensor(lo[:, :, 0:D], src, hi[:, :, 0:D].bitcast(F32),
                                       ALU.subtract).then_inc(v_split, 1)
                    pool.wait_ge(v_split, g + 1)

                def normalise(g, p):
                    pool.wait_ge(rbc_in, g * 16 + 32)
                    pool.tensor_tensor(o_raw[p][0:D, :], o_raw[p][0:D, :], rbc[:], ALU.mult).then_inc(norm_done, 1)
                    pool.wait_ge(norm_done, g + 2)

                def body(i, last):
                    for j in range(STEPS):
                        p, t = divmod(j, KT)
                        if t + 1 in POOL_T:
                            make_low(pool, i, j + 1, pl_pool)
                        if p == 1 and t == 8 and not last:
                            pool.wait_ge(pv_done, PB + (2 * i + 1) * KT)
                            split_v(i + 1, 0)
                        if p == 1 and t == 12:
                            normalise(2 * i, 0)
                        if p == 0 and t == 8:
                            pool.wait_ge(pv_done, PB + 2 * i * KT)
                            split_v(i, 1)
                        if p == 0 and t == 12:
                            normalise(2 * i - 1, 1)

                for p in range(2):
                    pool.memset(kb[p][3 * 32:SHIFT + 1, :].bitcast(F32), 1.0).then_inc(ones_done, 1)
                pool.wait_ge(ones_done, 2)
                for p in range(2):
                    pool.memset(v_s[p][0][:, :, D:DA].bitcast(F32), 1.0).then_inc(ones_done, 1)
                    pool.memset(v_s[p][1][:, :, D:DA].bitcast(F32), 0.0).then_inc(ones_done, 1)
                pool.memset(one[:], 1.0).then_inc(ones_done, 1)
                pool.wait_ge(ones_done, 7)
                pool.memset(rbc[:], 1.0).then_inc(rbc_in, 16)
                pool.wait_ge(rbc_in, 16)
                pool.memset(o_raw[1][0:D, :], 1.0).then_inc(ones_done, 1)
                pool.wait_ge(ones_done, 8)
                split_v(0, 0)
                both(pool, body)
                normalise(G - 1, 1)

            @block.scalar
            def _(act):
                def exp(i, j, before=None, between=lambda: None):
                    n, r = i * STEPS + j, keys(j % KT)
                    act.wait_ge(s_full, n + 1)
                    if j >= PF:
                        wait_low(act, i, j - PF)
                    elif before is not None:
                        wait_low(act, before, j - PF + STEPS)
                    act.activation(prob[j % PF][0:r, :], s_ps[j % 2][0:r, :], ACT.Exp, scale=SCALE
                                   ).then_inc(e_done, 1)
                    between()
                    act.wait_ge(e_done, n + 1)
                    act.wait_ge(pv_done, n + 1)
                    act.activation(ph[j % PB][0:r, :], prob[j % PF][0:r, :], ACT.Copy).then_inc(ph_done, 1)

                def take(i, p):
                    g = 2 * i + p
                    act.wait_ge(pv_done, PB + (g + 1) * KT)
                    act.wait_ge(hs_out[p], (i + 1) * 16)
                    act.activation(o_raw[p][:], o_ps[:], ACT.Copy).then_inc(o_act, 1)

                def body(i, last):
                    for j in range(STEPS):
                        ends = j % KT == KT - 1
                        between = (lambda: take(i, j // KT)) if ends else (lambda: None)
                        if j + 2 < STEPS:
                            exp(i, j + 2, between=between)
                        elif not last:
                            exp(i + 1, j + 2 - STEPS, i, between)
                        else:
                            between()

                act.sem_inc(o_act, 1)
                for p in range(2):
                    act.sem_inc(hs_out[p], 16)
                exp(0, 0)
                exp(0, 1)
                both(act, body)

            @block.vector
            def _(dve):
                def split(i, j):
                    if j % KT not in POOL_T:
                        make_low(dve, i, j, pl_dve)

                def piece(i, p, k):
                    n = (2 * i + p) * MXN + k
                    qt, c = divmod(k, SKV // CH)
                    w = min(CH, SK - c * CH)
                    dve.wait_ge(mx_full, n + 1)
                    dve.tensor_reduce(mpart[:, p, qt, c:c + 1], mx_ps[k % 2][:, 0:w], AX, ALU.max).then_inc(mx_done, 1)

                def top(i, p):
                    g = 2 * i + p
                    dve.wait_ge(mx_done, (g + 1) * MXN)
                    dve.tensor_reduce(mtop[:, p, :], mpart[:, p], AX, ALU.max).then_inc(mtop_done, 1)
                    dve.wait_ge(mtop_done, g + 1)
                    dve.tensor_scalar(mneg[:, p, :], mtop[:, p, :], -1.0, None, ALU.mult).then_inc(neg_done, 1)
                    dve.wait_ge(neg_done, g + 1)

                def invert(p, count):
                    dve.wait_ge(den_in[p], count * 16)
                    dve.reciprocal(rden[p][:], den[p][:]).then_inc(rden_done[p], 1)

                def body(i, last):
                    for j in range(STEPS):
                        p, t = divmod(j, KT)
                        todo = [] if last and p else list(pieces(t))
                        for k in todo[:SPLIT_AT]:
                            piece(i + p, 1 - p, k)
                        if j + 1 < STEPS:
                            split(i, j + 1)
                        elif not last:
                            split(i + 1, 0)
                        for k in todo[SPLIT_AT:]:
                            piece(i + p, 1 - p, k)
                        if todo and todo[-1] == MXN - 1:
                            top(i + p, 1 - p)
                        if j == 3:
                            invert(1, i + 1)
                        if j == KT + 3:
                            invert(0, i + 1)

                dve.memset(den[1][:], 1.0).then_inc(den_in[1], 16)
                for k in range(MXN):
                    piece(0, 0, k)
                top(0, 0)
                split(0, 0)
                both(dve, body)
                invert(1, G // 2 + 1)

            @block.tensor
            def _(pe):
                def piece(i, p, k):
                    n = (2 * i + p) * MXN + k
                    qt, c = divmod(k, SKV // CH)
                    w = min(CH, SK - c * CH)
                    if k == 0:
                        pe.wait_ge(qk_in[p], (i + 1) * 64)
                    if k >= 2 or not isinstance(i, int) or i or p:
                        pe.wait_ge(mx_done, n - 1)
                    pe.matmul(mx_ps[k % 2][:, 0:w], qa[p][:, qt:SQ:ST], ka[p][:, c * CH:c * CH + w],
                              start=True, stop=True).then_inc(mx_full, 1)

                def scores(i, j, between):
                    n = i * STEPS + j
                    p, t = divmod(j, KT)
                    r = keys(t)
                    if t == 0:
                        pe.wait_ge(qk_in[p], (i + 1) * 64)
                        pe.wait_ge(qkb_in[p], (i + 1) * 64)
                        pe.wait_ge(neg_in[p], (i + 1) * 16)
                    if not (isinstance(i, int) and i == 0 and j < 2):
                        pe.wait_ge(e_done, n - 1)
                    for a, y, first in ((ka[p], qa[p], True), (kb[p], qb[p], False)):
                        rows = P if first else SHIFT + 1
                        for u in range(2):
                            mm = pe.matmul(s_ps[j % 2][0:r, u * CH:(u + 1) * CH], a[0:rows, t * P:t * P + r],
                                           y[0:rows, u * CH:(u + 1) * CH], start=first, stop=not first)
                        if first:
                            between()
                    mm.then_inc(s_full, 1)

                def values(i, j, between):
                    n = i * STEPS + j
                    p, t = divmod(j, KT)
                    r = keys(t)
                    if t == 0:
                        pe.wait_ge(v_split, 2 * i + p + 1)
                        pe.wait_ge(o_act, 2 * i + p + 1)
                    wait_low(pe, i, j)
                    hi, lo = v_s[p]
                    for m, (a, y) in enumerate(((hi, ph), (lo, ph), (hi, pl))):
                        for u in range(2):
                            mm = pe.matmul(o_ps[:, u * CH:(u + 1) * CH], a[0:r, t, :],
                                           y[j % PB][0:r, u * CH:(u + 1) * CH],
                                           start=t == 0 and m == 0, stop=t == KT - 1 and m == 2)
                        if m < 2:
                            between()
                    mm.then_inc(pv_done, 1)

                def body(i, last):
                    for j in range(STEPS):
                        p, t = divmod(j, KT)
                        todo = [] if last and p else list(pieces(t))

                        def between():
                            if todo:
                                piece(i + p, 1 - p, todo.pop(0))

                        if j + 2 < STEPS:
                            scores(i, j + 2, between)
                        elif not last:
                            scores(i + 1, j + 2 - STEPS, between)
                        values(i, j, between)
                        assert not todo

                pe.sem_inc(pv_done, PB)
                for k in range(MXN):
                    piece(0, 0, k)
                pe.wait_ge(ones_done, 7)
                for j in range(2):
                    scores(0, j, lambda: None)
                both(pe, body)


def pieces(t):
    assert sum(PIECES) == MXN
    return range(sum(PIECES[:t]), sum(PIECES[:t + 1]))


def output(nc, kept, d, scratch, out):
    with ExitStack() as stack:
        s = Scope(nc, stack)
        wout_f = s.sb("o_wout_f", [P, MC, HID])
        wout = (s.sb("o_wout_hi", [P, MC, HID], F32R), s.sb("o_wout_lo", [P, MC, HID], F32R))
        bias = s.sb("o_bias", [P, HID])
        p2 = s.sb("o_p2", [HT, 1, SQ])
        hs_f = [s.sb(f"o_hs_f{p}", [P, MC, P]) for p in range(2)]
        hs_s = [(s.sb(f"o_hs_hi{p}", [P, MC, P], F32R), s.sb(f"o_hs_lo{p}", [P, MC, P], F32R)) for p in range(2)]
        x_t = [s.sb(f"o_x{p}", [P, HID]) for p in range(2)]
        o_t = [s.sb(f"o_o{p}", [P, HID]) for p in range(2)]
        ps = [s.psum(f"o_ps{p}", [P, 2, CH]) for p in range(2)]

        w_in, w_hi, w_lo, bias_in = s.sem("o_w_in"), s.sem("o_w_hi"), s.sem("o_w_lo"), s.sem("o_bias_in")
        hs_in = [s.sem(f"o_hs_in{p}") for p in range(2)]
        x_in = [s.sem(f"o_x_in{p}") for p in range(2)]
        hi, lo, p2_done = s.sem("o_hi"), s.sem("o_lo"), s.sem("o_p2_done")
        xb, full = s.sem("o_xb"), s.sem("o_full")
        done = s.sem("o_done")
        o_out = [s.sem(f"o_out{p}") for p in range(2)]
        C = 2
        hs_v = scratch["hs"].rearrange("(b m p) q -> b p m q", m=MC, p=P)

        with nc.Block() as block:
            @block.sync
            def _(sp):
                sp.dma_start(wout_f[:], d["wout"].rearrange("(m p) n -> p m n", p=P)).then_inc(w_in, 16)
                sp.dma_start(bias[:], d["bias"].to_broadcast([P, HID])).then_inc(bias_in, 16)
                with sp.Fori(0, B) as b:
                    for t in range(ST):
                        n, p = b * ST + t, t % 2
                        sp.wait_ge(lo, n + 1)
                        sp.dma_start(hs_f[p][:], hs_v[bass.ds(b, 1), :, :, t * P:(t + 1) * P]
                                     .rearrange("o p m q -> p (o m) q")).then_inc(hs_in[p], 16)
                        sp.wait_ge(done, n + 1)
                        sp.dma_start(x_t[p][:], d["x"].rearrange("b s n -> (b s) n")[bass.ds(b * SQ + t * P, P), :]
                                     ).then_inc(x_in[p], 16)

            @block.gpsimd
            def _(pool):
                pool.wait_ge(bias_in, 16)
                with pool.Fori(0, B) as b:
                    for t in range(ST):
                        n, p = b * ST + t, t % 2
                        pool.wait_ge(x_in[p], (b * (ST // 2) + t // 2 + 1) * 16)
                        pool.tensor_tensor(x_t[p][:], x_t[p][:], bias[:], ALU.add).then_inc(xb, 1)

            @block.scalar
            def _(act):
                for p in range(2):
                    act.sem_inc(o_out[p], 16)
                act.wait_ge(w_in, 16)
                act.activation(wout[0][:], wout_f[:], ACT.Copy).then_inc(w_hi, 1)

                def split(b, t):
                    n, p = b * ST + t, t % 2
                    act.wait_ge(hs_in[p], (b * (ST // 2) + t // 2 + 1) * 16)
                    act.wait_ge(full, n + 1)
                    act.activation(hs_s[p][0][:], hs_f[p][:], ACT.Copy).then_inc(hi, 1)

                with act.Fori(0, B) as b:
                    act.wait_ge(full, b * ST + C)
                    act.activation(p2[:], kept["p2g"][:, bass.ds(b, 1), :], ACT.Copy).then_inc(p2_done, 1)
                    split(b, 0)
                    for t in range(ST):
                        if t + 1 < ST:
                            split(b, t + 1)
                        n, p = b * ST + t, t % 2
                        act.wait_ge(done, n + 1 + C)
                        act.dma_start(out[bass.ds(b * SQ + t * P, P), :], o_t[p][:]).then_inc(o_out[p], 16)
                for p in range(2):
                    act.wait_ge(o_out[p], 16 + 16 * B * ST // 2)

            @block.vector
            def _(dve):
                dve.sem_inc(lo, C)
                dve.sem_inc(done, C)
                dve.wait_ge(w_hi, 1)
                dve.tensor_tensor(wout[1][:], wout_f[:], wout[0][:].bitcast(F32), ALU.subtract).then_inc(w_lo, 1)

                def split(b, t):
                    n, p = b * ST + t, t % 2
                    dve.wait_ge(hi, n + 1)
                    dve.tensor_tensor(hs_s[p][1][:], hs_f[p][:], hs_s[p][0][:].bitcast(F32),
                                      ALU.subtract).then_inc(lo, 1)

                with dve.Fori(0, B) as b:
                    split(b, 0)
                    for t in range(ST):
                        if t + 1 < ST:
                            split(b, t + 1)
                        n, p = b * ST + t, t % 2
                        dve.wait_ge(full, n + 1 + C)
                        dve.wait_ge(xb, n + 1)
                        dve.wait_ge(o_out[p], (b * (ST // 2) + t // 2 + 1) * 16)
                        u = lambda a: a.rearrange("p (u n) -> p u n", u=2)
                        dve.tensor_tensor(u(o_t[p][:]), ps[p][:, :, 0:HALF], u(x_t[p][:]), ALU.add).then_inc(done, 1)

            @block.tensor
            def _(pe):
                pe.sem_inc(full, C)
                pe.wait_ge(w_lo, 1)
                with pe.Fori(0, B) as b:
                    pe.wait_ge(p2_done, b + 1)
                    for t in range(ST):
                        n, p = b * ST + t, t % 2
                        pe.wait_ge(lo, n + 1 + C)
                        pe.wait_ge(done, n + 1)
                        for m in range(MC):
                            for i, (a, y) in enumerate(products(hs_s[p], wout)):
                                for u in range(2):
                                    pe.matmul(ps[p][:, u, 0:HALF], a[:, m, :], y[:, m, u * HALF:(u + 1) * HALF],
                                              start=m == 0 and i == 0, stop=False)
                        for u in range(2):
                            mm = pe.matmul(ps[p][:, u, 0:HALF], p2[:, 0, t * P:(t + 1) * P],
                                           kept["vw"][:, bass.ds(b, 1), u * HALF:(u + 1) * HALF], start=False, stop=True)
                        mm.then_inc(full, 1)


def program(nc, d, out):
    dram = lambda name, shape: nc.dram_tensor(name, shape, F32, kind="Internal").ap()
    scratch = {
        "kh": dram("k_hi_d", [B * HID, SKV]), "kl": dram("k_lo_d", [B * HID, SKV]),
        "qh": dram("q_hi_d", [B * HID, SQ]), "ql": dram("q_lo_d", [B * HID, SQ]),
        "v": dram("v_d", [G, P, KT * D]), "hs": dram("heads_d", [B * HID, SQ]), "rden": dram("rden_d", [G, SQ]),
    }
    with ExitStack() as stack:
        s = Scope(nc, stack)
        kept = {
            "u": s.sb("u", [3 * HT + 1, B * SQ], F32R),
            "wk2": s.sb("wk2", [DA, B, NH, HT + 2]),
            "vw": s.sb("vw", [HT, B, HID]),
            "p2g": s.sb("p2g", [HT, B, SQ]),
            "u_ones": s.sem("u_ones"),
            "ntop": s.sb("ntop", [P, B, NH * KC], F32R),
        }
        with ExitStack() as inner:
          kept["ca1"] = Scope(nc, inner).sb("ca1", [P, NH * CD], F32R)
          with ExitStack() as winner:
            ws = Scope(nc, winner)
            pair = lambda n, k, c: (ws.sb(f"{n}_hi", [P, k, c], F32R), ws.sb(f"{n}_lo", [P, k, c], F32R))
            w = {"wq": pair("wq", MC, HID), "wk": pair("wk", KC, HID), "wv": pair("wv", KC, HID),
                 "wqca": pair("wqca", MC, K3)}
            project(nc, kept, w, d, scratch)
          tokens(nc, kept, d)
        attend(nc, kept, scratch)
        output(nc, kept, d, scratch, out.rearrange("b s n -> (b s) n"))


def layouts(x, ctx, Wq, Wk, Wv, Wq_ca, Wk_ca, Wv_ca, Wout, b_out):
    ca = ctx[:, SK:, :]
    wqca = np.zeros((NH, D, 3, NH, NT), Wq_ca.dtype)
    ca_bd = np.zeros((B, 3, NH, NT, NH, CD), ctx.dtype)
    for h in range(NH):
        for r in range(3):
            wqca[h, :, r, h, :] = Wq_ca[:, h * D:(h + 1) * D].T
            ca_bd[:, r, h, :, h, :] = ca
    mask = np.zeros((NH, D, NH), np.float32)
    for h in range(NH):
        mask[h, :, h] = 1
    frame = np.zeros((DA, B, NH, HT + 2), np.float32)
    frame[D, :, :, HT] = 1
    onehot = np.zeros((P, SQ), np.float32)
    onehot[gather_index() % P, np.arange(SQ)] = 1
    return {
        "x": x, "xT": x.transpose(0, 2, 1), "ctxT": ctx.transpose(0, 2, 1),
        "wq": Wq, "wqT": Wq.T, "wk": Wk, "wv": Wv, "wkca": Wk_ca, "wvca": Wv_ca, "wout": Wout,
        "bias": b_out.reshape(1, HID), "caT": ca.transpose(2, 0, 1).reshape(CD, B * NT),
        "wqca": wqca.reshape(HID, 3 * HT), "caBD": ca_bd.reshape(B, 3 * HT, NH * CD),
        "mask": mask.reshape(HID, NH), "wk2_frame": frame, "onehot": onehot,
    }


def kernel(x, ctx_768, L0_xattn_Wq, L0_xattn_Wk, L0_xattn_Wv, L0_xattn_Wq_ca, L0_xattn_Wk_ca,
           L0_xattn_Wv_ca, L0_xattn_Wout, L0_xattn_b_out):
    import concourse.bacc as bacc
    from concourse.bass_utils import run_bass_kernel_spmd

    a = [np.asarray(v) for v in (x, ctx_768, L0_xattn_Wq, L0_xattn_Wk, L0_xattn_Wv, L0_xattn_Wq_ca,
                                 L0_xattn_Wk_ca, L0_xattn_Wv_ca, L0_xattn_Wout, L0_xattn_b_out)]
    nc = bacc.Bacc("TRN2", target_bir_lowering=False, num_devices=1)
    arrays, d = {}, {}
    for name, v in layouts(*a).items():
        arrays[f"in_{name}"] = np.ascontiguousarray(v)
        d[name] = nc.dram_tensor(f"in_{name}", v.shape, mybir.dt.from_np(v.dtype), kind="ExternalInput").ap()
    out = nc.dram_tensor("out", (B, SQ, HID), F32, kind="ExternalOutput").ap()
    program(nc, d, out)
    r = run_bass_kernel_spmd(nc, [arrays], core_ids=[0])
    return r.results[0]["out"]
```

```python
from contextlib import ExitStack

import concourse.bass as bass
from concourse import mybir
import numpy as np

F32 = mybir.dt.float32
F32R = mybir.dt.float32r
ALU = mybir.AluOpType
ACT = mybir.ActivationFunctionType
AX = mybir.AxisListType.X

P = 128
B, SQ, HID = 2, 1024, 640
SKV, CD, NT = 2048, 384, 4
SK = SKV - NT
NH = 8
D = HID // NH
SCALE = float(D) ** -0.5
MC, KC = HID // P, CD // P
HT = NH * NT
K3 = 3 * HT
CH = 512
HALF = HID // 2
KT = SKV // P
LASTK = SK - (KT - 1) * P
ST = SQ // P
G = B * NH
DA = D + 1
LO_A = P - D
LO_B = D - LO_A
SHIFT = D + LO_B

RING = 5
MAX_FROM = 6
PB = 4
PF = 4
MXN = ST * SKV // CH
PIECES = (2, 3, 2, 3, 3, 2, 3, 3, 2, 3, 3, 3)
POOL_T = (4,)
SPLIT_AT = 1


def gather_index():
    return np.linspace(0, CD - 1, SQ).astype(np.int64)


def products(a, b):
    return ((a[0], b[0]), (a[0], b[1]), (a[1], b[0]))


class Scope:

    def __init__(self, nc, stack):
        self.nc, self.stack = nc, stack

    def sb(self, name, shape, dt=F32):
        return self.stack.enter_context(self.nc.sbuf_tensor(name, shape, dt))

    def place_before(self, name, shape, dt=F32):
        with self.nc.sbuf_tensor(name, shape, dt) as t:
            return t

    def psum(self, name, shape, dt=F32):
        return self.stack.enter_context(self.nc.psum_tensor(name, shape, dt))

    def sem(self, name):
        return self.stack.enter_context(self.nc.semaphore(name))


class Heads:

    def __init__(self, s, spare, spare2):
        sb, sem = s.sb, s.sem
        self.ka = [sb(f"ka{p}", [P, SKV], F32R) for p in range(2)]
        self.qa = [sb(f"qa{p}", [P, SQ], F32R) for p in range(2)]
        self.kb = [sb("kb0", [P, SKV], F32R)]
        self.qb = [sb("qb0", [P, SQ], F32R)]
        self.v_f = sb("v_f", [P, 1, KT * D])
        self.v_s = [self.split_values(s, 0)]
        self.one = sb("one", [P, 1])
        self.mpart = sb("mpart", [P, 2, ST, SKV // CH])
        self.mtop = sb("mtop", [P, 2, ST])
        self.mneg = sb("mneg", [P, 2, ST], F32R)
        self.mx_ps = None

        self.qk_in = [sem(f"at_qk_in{p}") for p in range(2)]
        self.qkb_in = [sem(f"at_qkb_in{p}") for p in range(2)]
        self.neg_in = [sem(f"at_neg_in{p}") for p in range(2)]
        self.v_in, self.vh_done, self.v_split = sem("at_v_in"), sem("at_v_hi"), sem("at_v_split")
        self.one_done, self.kb_ones, self.v_ones = sem("at_one"), sem("at_kb_ones"), sem("at_v_ones")
        self.mx_full, self.mx_done = sem("at_mx_full"), sem("at_mx_done")
        self.mtop_done, self.neg_done = sem("at_mtop"), sem("at_neg")

        self.o_raw = [spare2[0:DA, 0:SQ], spare[0:DA, 0:SQ]]
        self.den = [None, sb("den1", [P, ST])]
        self.rden = [None, sb("rden1", [P, ST])]
        self.rbc = spare[0:D, SQ:2 * SQ]
        self.o_act = sem("at_o_act")
        self.den_in = [sem(f"at_den_in{p}") for p in range(2)]
        self.rden_done = [sem(f"at_rden{p}") for p in range(2)]
        self.rden_out, self.rbc_in, self.norm_done = sem("at_rden_out"), sem("at_rbc_in"), sem("at_norm")
        self.hs_out = [sem(f"at_hs_out{p}") for p in range(2)]

    @staticmethod
    def split_values(s, p):
        return s.sb(f"v_hi{p}", [P, KT, DA], F32R), s.sb(f"v_lo{p}", [P, KT, DA], F32R)

    def second(self, s):
        self.kb.append(s.sb("kb1", [P, SKV], F32R))
        self.qb.append(s.sb("qb1", [P, SQ], F32R))
        self.v_s.append(self.split_values(s, 1))
        self.den[0], self.rden[0] = s.sb("den0", [P, ST]), s.sb("rden0", [P, ST])

    def fill_ones(self, pool, p):
        pool.memset(self.kb[p][3 * 32:SHIFT + 1, :].bitcast(F32), 1.0).then_inc(self.kb_ones, 1)
        pool.wait_ge(self.kb_ones, p + 1)
        pool.memset(self.v_s[p][0][:, :, D:DA].bitcast(F32), 1.0).then_inc(self.v_ones, 1)
        pool.memset(self.v_s[p][1][:, :, D:DA].bitcast(F32), 0.0).then_inc(self.v_ones, 1)

    def load_a(self, sp, scratch, i, p):
        r = lambda off, n: bass.ds((2 * i + p) * D + off, n)
        f = lambda x: x.bitcast(F32)
        for dst, src in (
            (f(self.qa[p][0:D, :]), scratch["qh"][r(0, D), :]),
            (f(self.qa[p][D:P, :]), scratch["qh"][r(0, LO_A), :]),
            (f(self.ka[p][0:D, :]), scratch["kh"][r(0, D), :]),
            (f(self.ka[p][D:P, :]), scratch["kl"][r(0, LO_A), :]),
        ):
            sp.dma_start(dst, src).then_inc(self.qk_in[p], 16)

    def load_b(self, sp, scratch, i, p):
        r = lambda off, n: bass.ds((2 * i + p) * D + off, n)
        f = lambda x: x.bitcast(F32)
        for dst, src in (
            (f(self.qb[p][0:D, :]), scratch["ql"][r(0, D), :]),
            (f(self.qb[p][D:SHIFT, :]), scratch["qh"][r(LO_A, LO_B), :]),
            (f(self.kb[p][0:D, :]), scratch["kh"][r(0, D), :]),
            (f(self.kb[p][D:SHIFT, :]), scratch["kl"][r(LO_A, LO_B), :]),
        ):
            sp.dma_start(dst, src).then_inc(self.qkb_in[p], 16)

    def shift(self, sp, i, p):
        sp.wait_ge(self.neg_done, 2 * i + p + 1)
        sp.dma_start(self.qb[p][SHIFT:SHIFT + 1, :].rearrange("o (q g) -> o q g", q=P).bitcast(F32),
                     self.mneg[:, p, :].bitcast(F32)).then_inc(self.neg_in[p], 16)

    def split_v(self, pool, scratch, i, p):
        g = 2 * i + p
        hi, lo = self.v_s[p]
        pool.dma_start(self.v_f[:], scratch["v"][bass.ds(g, 1), :, :].rearrange("o p n -> p o n")
                       ).then_inc(self.v_in, 16)
        pool.wait_ge(self.v_in, (g + 1) * 16)
        src = self.v_f[:, 0, :].rearrange("p (t d) -> p t d", d=D)
        pool.tensor_tensor(hi[:, :, 0:D], src, self.one[:, :, None].to_broadcast([P, KT, D]),
                           ALU.mult).then_inc(self.vh_done, 1)
        pool.wait_ge(self.vh_done, g + 1)
        pool.tensor_tensor(lo[:, :, 0:D], src, hi[:, :, 0:D].bitcast(F32),
                           ALU.subtract).then_inc(self.v_split, 1)
        pool.wait_ge(self.v_split, g + 1)

    def score_piece(self, pe, i, p, k):
        n = (2 * i + p) * MXN + k
        qt, c = divmod(k, SKV // CH)
        w = min(CH, SK - c * CH)
        if k == 0:
            pe.wait_ge(self.qk_in[p], (i + 1) * 64)
        if k >= 2 or not isinstance(i, int) or i or p:
            pe.wait_ge(self.mx_done, n - 1)
        pe.matmul(self.mx_ps[k % 2][:, 0:w], self.qa[p][:, qt:SQ:ST], self.ka[p][:, c * CH:c * CH + w],
                  start=True, stop=True).then_inc(self.mx_full, 1)

    def max_piece(self, dve, i, p, k):
        n = (2 * i + p) * MXN + k
        qt, c = divmod(k, SKV // CH)
        w = min(CH, SK - c * CH)
        dve.wait_ge(self.mx_full, n + 1)
        dve.tensor_reduce(self.mpart[:, p, qt, c:c + 1], self.mx_ps[k % 2][:, 0:w], AX, ALU.max
                          ).then_inc(self.mx_done, 1)

    def top(self, dve, i, p):
        g = 2 * i + p
        dve.wait_ge(self.mx_done, (g + 1) * MXN)
        dve.tensor_reduce(self.mtop[:, p, :], self.mpart[:, p], AX, ALU.max).then_inc(self.mtop_done, 1)
        dve.wait_ge(self.mtop_done, g + 1)
        dve.tensor_scalar(self.mneg[:, p, :], self.mtop[:, p, :], -1.0, None, ALU.mult).then_inc(self.neg_done, 1)
        dve.wait_ge(self.neg_done, g + 1)

    def invert(self, dve, p, count):
        dve.wait_ge(self.den_in[p], count * 16)
        dve.reciprocal(self.rden[p][:], self.den[p][:]).then_inc(self.rden_done[p], 1)

    def spread(self, eng, scratch, i, p):
        g = 2 * i + p
        eng.wait_ge(self.o_act, g + 2)
        eng.dma_start(self.den[p][:], self.o_raw[p][D:DA, :].rearrange("o (p j) -> o p j", p=P)
                      ).then_inc(self.den_in[p], 16)
        eng.wait_ge(self.rden_done[p], i + 1 + p)
        eng.dma_start(scratch["rden"][bass.ds(g, 1), :].rearrange("o (p j) -> p (o j)", p=P),
                      self.rden[p][:]).then_inc(self.rden_out, 16)
        eng.wait_ge(self.rden_out, (g + 1) * 16)
        eng.wait_ge(self.norm_done, g + 1)
        eng.dma_start(self.rbc[:, None, :], scratch["rden"][None, bass.ds(g, 1), :].to_broadcast([D, 1, SQ])
                      ).then_inc(self.rbc_in, 16)

    def normalise(self, pool, g, p):
        pool.wait_ge(self.rbc_in, g * 16 + 32)
        pool.tensor_tensor(self.o_raw[p][0:D, :], self.o_raw[p][0:D, :], self.rbc[:], ALU.mult
                           ).then_inc(self.norm_done, 1)
        pool.wait_ge(self.norm_done, g + 2)

    def put(self, eng, scratch, g, p):
        eng.wait_ge(self.norm_done, g + 2)
        eng.dma_start(scratch["hs"][bass.ds(g * D, D), :], self.o_raw[p][0:D, :]).then_inc(self.hs_out[p], 16)


def project(nc, outer, kept, w, d, scratch):
    NS = SKV // CH
    NQ = SQ // CH
    with ExitStack() as stack:
        s = Scope(nc, stack)
        ctx_f = [s.sb(f"ctx_f{i}", [P, 1, KC, CH]) for i in range(2)]
        ctx_s = [(s.sb(f"ctx_hi{i}", [P, KC, CH], F32R), s.sb(f"ctx_lo{i}", [P, KC, CH], F32R)) for i in range(2)]
        x_f = kept["x_f"]
        ca_f = kept["ca_f"]
        ca = kept["ca1"]
        part = s.sb("pj_part", [P, NH * KC, 2])
        top = s.sb("pj_top", [P, NH * KC])
        x_s = (kept["x_hi"], s.sb("x_lo", [P, MC, CH], F32R))
        ring, v_t = w["ring"], w["v_t"]
        banks = [s.psum(f"bank{i}", [P, CH]) for i in range(8)]
        u_all = kept["u"]

        ctx_in = [s.sem(f"pj_ctx_in{i}") for i in range(2)]
        ctx_hi, ctx_lo = s.sem("pj_ctx_hi"), s.sem("pj_ctx_lo")
        x_in, x_hi, x_lo = s.sem("pj_x_in"), s.sem("pj_x_hi"), s.sem("pj_x_lo")
        full, hi_done, done = s.sem("pj_full"), s.sem("pj_hi"), s.sem("pj_done")
        ring_out = [outer.sem(f"pj_ring_out{i}") for i in range(RING)]
        v_out = [outer.sem(f"pj_v_out{i}") for i in range(2)]

        w_in = [s.sem(f"pj_w_in{n}") for n in range(4)]
        ctx0_in, x0_in = s.sem("pj_ctx0_in"), s.sem("pj_x0_in")
        w_hi, w_lo = s.sem("pj_w_hi"), s.sem("pj_w_lo")
        ca_in, ca_hi, ca_lo = s.sem("pj_ca_in"), s.sem("pj_ca_hi"), s.sem("pj_ca_lo")
        top_done = s.sem("pj_top_done")
        flat = v_t[:].rearrange("p a h t d -> p (a h t d)")
        n_k = KC * HID
        stages = [("wk", flat[:, 0:n_k]), ("wv", flat[:, n_k:2 * n_k]),
                  ("wqca", flat[:, 2 * n_k:2 * n_k + MC * K3]), ("wq", ca_f[:])]
        stages = [(n, v.rearrange("p (m n) -> p m n", m=w[n][0].shape[1])) for n, v in stages]

        jobs, maxima = [], [("m", 0, (hc, u)) for hc in range(NH * KC) for u in range(2)]
        for c in range(NS):
            for job in [("k", c, m) for m in range(MC)] + [("v", c, (t, u)) for t in range(4) for u in range(2)]:
                jobs.append(job)
                if c >= NQ:
                    some = 3 if job[0] == "k" else 2
                    jobs += maxima[:some]
                    maxima = maxima[some:]
            if c < NQ:
                jobs += [("q", c, m) for m in range(MC)] + [("u", c, 0)]
        assert not maxima
        NJ = len(jobs)
        assert NJ % 8 == 0
        split_jobs = [j for j in jobs if j[0] in "kqu"]
        ring_jobs = [j for j in jobs if j[0] in "kq"]
        last = {(kind, c): n for n, (kind, c, _) in enumerate(jobs)}
        last_m = last["m", 0]

        def read_ctx(c):
            return last["v", c] + 1 + NJ if c >= 0 else last["v", c + NS] + 1

        def read_x(c):
            return last["u", c] + 1 + NJ if c >= 0 else last["u", c + NQ] + 1

        NSP, NR = len(split_jobs), len(ring_jobs)
        assert NR % RING == 0

        ctxT = d["ctxT"].rearrange("b (m p) s -> p b m s", p=P)
        xT = d["xT"].rearrange("b (m p) s -> p b m s", p=P)

        with nc.Block() as block:
            @block.gpsimd
            def _(pool):
                pool.sem_inc(ctx_lo, 2)
                pool.sem_inc(x_lo, 1)
                pool.sem_inc(ca_lo, 1)
                pool.memset(u_all[K3:K3 + 1, :].bitcast(F32), 1.0).then_inc(kept["u_ones"], 1)
                for b in range(B):
                    for c in range(NS):
                        if b == 0 and c == 1:
                            pool.wait_ge(w_in[3], 16)
                        pool.wait_ge(ctx_lo, b * NS + c + 1)
                        if b or c:
                            pool.dma_start(ctx_f[c % 2][:], ctxT[:, b:b + 1, :, c * CH:(c + 1) * CH]
                                           ).then_inc(ctx_in[c % 2], 16)
                        if c < NQ and (b or c):
                            q = c
                            if b == 0:
                                pool.wait_ge(full, last["v", 0] + 1 + NJ)
                            pool.wait_ge(x_lo, b * NQ + q + 1)
                            pool.dma_start(x_f[:], xT[:, bass.ds(b, 1), :, q * CH:(q + 1) * CH]
                                           ).then_inc(x_in, 16)
                        if c == 1:
                            pool.wait_ge(w_lo, len(stages))
                            pool.wait_ge(ca_lo, b + 1)
                            pool.dma_start(ca_f[0:K3, None, 0:NH * CD], d["caBD"].rearrange("b k n -> k b n")
                                           [:, bass.ds(b, 1), :]).then_inc(ca_in, 16)

            @block.sync
            def _(sp):
                for n, (name, stage) in enumerate(stages):
                    sp.dma_start(stage, d[name].rearrange("(m p) n -> p m n", p=P)).then_inc(w_in[n], 16)
                    if name == "wk":
                        sp.dma_start(ctx_f[0][:], ctxT[:, 0:1, :, 0:CH]).then_inc(ctx0_in, 16)
                    if name == "wqca":
                        sp.dma_start(x_f[:], xT[:, 0:1, :, 0:CH]).then_inc(x0_in, 16)
                for b in range(B):
                    nr = ns = 0
                    for n, (kind, c, m) in enumerate(jobs):
                        if b == B - 1 and n == last_m + 2:
                            sp.wait_ge(top_done, 2 * B)
                            shift_tokens(sp, kept, ca, b)
                        if (b, kind, c, m) == (B - 1, "k", NQ, 0):
                            sp.wait_ge(full, b * NJ + read_x(NQ - 1))
                            sp.wait_ge(x_lo, B * NQ + 1)
                            x1 = d["x_ones"].rearrange("b (t p) (h d) -> b p t h d", p=P, d=DA)[B - 1]
                            for t in range(ST):
                                sp.dma_start(kept["xn1"][:, t], x1[:, t]).then_inc(kept["xn1_in"][t // 2], 16)
                            for name in ("wkca", "caT", "mask", "wvca"):
                                sp.dma_start(kept[name], d[name].rearrange("(m p) n -> p m n", p=P)
                                             ).then_inc(kept["small_in"], 16)
                            sp.wait_ge(ca_lo, B + 1)
                            sp.dma_start(kept["ca_f"][0:K3, 0:NH * CD], d["caBD"][0]).then_inc(kept["ca0_in"], 16)
                        if kind in "kq":
                            hi, lo = ring[nr % RING]
                            to = scratch["kh"], scratch["kl"]
                            if kind == "q":
                                to = scratch["qh"], scratch["ql"]
                            at = (bass.ds(b * HID + m * P, P), slice(c * CH, (c + 1) * CH))
                            sp.wait_ge(hi_done, b * NSP + ns + 1)
                            sp.dma_start(to[0][at], hi[:].bitcast(F32)).then_inc(ring_out[nr % RING], 16)
                            sp.wait_ge(done, b * NJ + n + 1 + 8)
                            sp.dma_start(to[1][at], lo[:].bitcast(F32)).then_inc(ring_out[nr % RING], 16)
                            nr += 1
                        if kind in "kqu":
                            ns += 1
                        if kind == "v" and m == (3, 1):
                            sp.wait_ge(done, b * NJ + n + 1 + 8)
                            sp.dma_start(scratch["v"][bass.ds(b * NH, NH), :, c * 4 * D:(c + 1) * 4 * D]
                                         .rearrange("h p n -> p h n"),
                                         v_t[:, c % 2].rearrange("p h t d -> p h (t d)")).then_inc(v_out[c % 2], 16)
            @block.scalar
            def _(act):
                for i in range(RING):
                    act.sem_inc(ring_out[i], 32)

                def split_ctx(b, c):
                    if b or c:
                        act.wait_ge(ctx_in[c % 2], (b * (NS // 2) + c // 2 + c % 2) * 16)
                    else:
                        act.wait_ge(ctx0_in, 16)
                    act.wait_ge(full, b * NJ + read_ctx(c - 2))
                    act.activation(ctx_s[c % 2][0][:], ctx_f[c % 2][:, 0], ACT.Copy).then_inc(ctx_hi, 1)

                def split_x(b, q):
                    if b or q:
                        act.wait_ge(x_in, (b * NQ + q) * 16)
                    else:
                        act.wait_ge(x0_in, 16)
                    act.wait_ge(full, b * NJ + read_x(q - 1))
                    act.activation(x_s[0][:], x_f[:, 0], ACT.Copy).then_inc(x_hi, 1)

                def split_ca(b):
                    act.wait_ge(ca_in, (b + 1) * 16)
                    act.wait_ge(full, b * NJ + NJ)
                    act.activation(ca[0:K3, :], ca_f[0:K3, 0:NH * CD], ACT.Copy).then_inc(ca_hi, 1)

                for n, (name, stage) in enumerate(stages):
                    act.wait_ge(w_in[n], 16)
                    act.activation(w[name][0][:], stage, ACT.Copy).then_inc(w_hi, 1)
                    if name == "wk":
                        split_ctx(0, 0)
                    if name == "wqca":
                        split_x(0, 0)
                for b in range(B):
                    nr = 0
                    if b:
                        split_ctx(b, 0)
                        split_x(b, 0)
                    for n, (kind, c, m) in enumerate(jobs):
                        if kind == "k" and m == 0 and c < NS - 1:
                            split_ctx(b, c + 1)
                        if kind == "k" and m == 0 and c == 1:
                            split_x(b, 1)
                        if kind == "q" and m == 0 and c == 1:
                            split_ca(b)
                        if kind in "vm":
                            continue
                        act.wait_ge(full, b * NJ + n + 1 + NJ)
                        if kind == "u":
                            dst = u_all[0:K3, bass.ds(b * SQ + c * CH, CH)]
                            act.activation(dst, banks[n % 8][0:K3, :], ACT.Copy).then_inc(hi_done, 1)
                        else:
                            act.wait_ge(ring_out[nr % RING], (b * (NR // RING) + nr // RING + 1) * 32)
                            act.activation(ring[nr % RING][0][:], banks[n % 8][:], ACT.Copy).then_inc(hi_done, 1)
                            nr += 1

            @block.vector
            def _(dve):
                for i in range(2):
                    dve.sem_inc(v_out[i], 16)

                def split_ctx(b, c):
                    dve.wait_ge(ctx_hi, b * NS + c + 1)
                    hi, lo = ctx_s[c % 2]
                    dve.tensor_tensor(lo[:], ctx_f[c % 2][:, 0], hi[:].bitcast(F32), ALU.subtract).then_inc(ctx_lo, 1)

                def split_x(b, q):
                    dve.wait_ge(x_hi, b * NQ + q + 1)
                    hi, lo = x_s
                    dve.tensor_tensor(lo[:], x_f[:, 0], hi[:].bitcast(F32), ALU.subtract).then_inc(x_lo, 1)

                def split_ca(b):
                    dve.wait_ge(ca_hi, b + 1)
                    rows = slice(HT, 2 * HT)
                    dve.tensor_tensor(ca[rows, :], ca_f[rows, 0:NH * CD], ca[rows, :].bitcast(F32),
                                      ALU.subtract).then_inc(ca_lo, 1)

                def negate_top(b):
                    dve.wait_ge(done, b * NJ + last_m + 1 + 8)
                    dve.tensor_reduce(top[:], part[:], AX, ALU.max).then_inc(top_done, 1)
                    dve.wait_ge(top_done, b * 2 + 1)
                    dve.tensor_scalar(kept["ntop"][:, b, :], top[:], -1.0, None, ALU.mult).then_inc(top_done, 1)
                    dve.wait_ge(top_done, b * 2 + 2)

                for n, (name, stage) in enumerate(stages):
                    dve.wait_ge(w_hi, n + 1)
                    dve.tensor_tensor(w[name][1][:], stage, w[name][0][:].bitcast(F32),
                                      ALU.subtract).then_inc(w_lo, 1)
                    if name == "wk":
                        split_ctx(0, 0)
                    if name == "wqca":
                        split_x(0, 0)
                dve.wait_ge(w_lo, len(stages))
                for b in range(B):
                    nr = ns = 0
                    if b:
                        split_ctx(b, 0)
                        split_x(b, 0)
                    for n, (kind, c, m) in enumerate(jobs):
                        if kind == "k" and m == 0 and c < NS - 1:
                            split_ctx(b, c + 1)
                        if kind == "k" and m == 0 and c == 1:
                            split_x(b, 1)
                        if kind == "q" and m == 0 and c == 1:
                            split_ca(b)
                        bank = banks[n % 8]
                        if kind == "m":
                            hc, u = m
                            dve.wait_ge(full, b * NJ + n + 1 + NJ)
                            dve.tensor_reduce(part[:, hc, u:u + 1], bank[:], AX, ALU.max).then_inc(done, 1)
                            if n == last_m:
                                negate_top(b)
                            continue
                        if kind == "v":
                            t, u = m
                            dve.wait_ge(full, b * NJ + n + 1 + NJ)
                            if t == 0 and u == 0:
                                dve.wait_ge(v_out[c % 2], (b * (NS // 2) + c // 2 + 1) * 16)
                            dve.tensor_copy(v_t[:, c % 2, u * 4:(u + 1) * 4, t, :],
                                            bank[:, 0:HALF].rearrange("p (h d) -> p h d", d=D)).then_inc(done, 1)
                            continue
                        dve.wait_ge(hi_done, b * NSP + ns + 1)
                        if kind == "u":
                            dst = u_all[2 * HT:K3, bass.ds(b * SQ + c * CH, CH)]
                            dve.tensor_tensor(dst, bank[2 * HT:K3, :], dst.bitcast(F32),
                                              ALU.subtract).then_inc(done, 1)
                        else:
                            hi, lo = ring[nr % RING]
                            dve.tensor_tensor(lo[:], bank[:], hi[:].bitcast(F32), ALU.subtract).then_inc(done, 1)
                            nr += 1
                        ns += 1

            @block.tensor
            def _(pe):
                pe.sem_inc(done, 8)
                pe.sem_inc(full, NJ)
                for b in range(B):
                    for n, (kind, c, m) in enumerate(jobs):
                        bank = banks[n % 8]
                        if b == 0 and c == 0 and m in (0, (0, 0)) and kind != "m":
                            pe.wait_ge(w_lo, {"k": 1, "v": 2, "q": 4, "u": 4}[kind])
                        if kind == "k" and m == 0:
                            pe.wait_ge(ctx_lo, b * NS + c + 1 + 2)
                        if kind == "q" and m == 0:
                            pe.wait_ge(x_lo, b * NQ + c + 1 + 1)
                        pe.wait_ge(done, b * NJ + n + 1)
                        if kind == "m":
                            hc, u = m
                            if (hc, u) == (0, 0):
                                pe.wait_ge(ca_lo, b + 2)
                                pe.wait_ge(done, b * NJ + last["u", NQ - 1] + 1 + 8)
                            at = hc // KC * CD + hc % KC
                            pe.matmul(bank[:], ca[0:K3, at:at + (P - 1) * KC + 1:KC],
                                      u_all[0:K3, bass.ds(b * SQ + u * CH, CH)], start=True, stop=True
                                      ).then_inc(full, 1)
                            continue
                        nk = {"k": KC, "v": KC, "q": MC, "u": MC}[kind]
                        mm = None
                        for k in range(nk):
                            if kind == "k":
                                pairs = [(a[:, k, m * P:(m + 1) * P], y[:, k, :])
                                         for a, y in products(w["wk"], ctx_s[c % 2])]
                                to = bank[:]
                            elif kind == "v":
                                t, u = m
                                pairs = [(a[:, k, t * P:(t + 1) * P], y[:, k, u * HALF:(u + 1) * HALF])
                                         for a, y in products(ctx_s[c % 2], w["wv"])]
                                to = bank[:, 0:HALF]
                            elif kind == "q":
                                pairs = [(a[:, k, m * P:(m + 1) * P], y[:, k, :]) for a, y in products(w["wq"], x_s)]
                                to = bank[:]
                            else:
                                pairs = [(a[:, k, :], y[:, k, :]) for a, y in products(w["wqca"], x_s)]
                                to = bank[0:K3, :]
                            for i, (a, y) in enumerate(pairs):
                                mm = pe.matmul(to, a, y, start=k == 0 and i == 0, stop=k == nk - 1 and i == 2)
                        mm.then_inc(full, 1)

        def written(eng):
            for i in range(RING):
                eng.wait_ge(ring_out[i], 32 + B * NR // RING * 32)
            for i in range(2):
                eng.wait_ge(v_out[i], 16 + B * NS // 2 * 16)

        return written


def shift_tokens(sp, kept, ca, b):
    for h in range(NH):
        row = ca[K3:K3 + 1, h * CD:(h + 1) * CD].rearrange("o (p c) -> o p c", c=KC)
        sp.dma_start(row.bitcast(F32), kept["ntop"][:, b, h * KC:(h + 1) * KC].bitcast(F32)
                     ).then_inc(kept["ntop_in"][b], 16)


def tokens(nc, kept, at, written, d, scratch):
    with ExitStack() as stack:
        s = Scope(nc, stack)
        wqT = s.sb("wqT", [P, MC, HID])
        wout = wqT
        wkca, wvca, caT, mask = kept["wkca"], kept["wvca"], kept["caT"], kept["mask"]
        tok = [s.sb(f"tok{i}", [P, MC, B * NT]) for i in range(2)]
        bd = [s.sb("bd0", [P, MC, B, NH, NT]), s.sb("bd1", [P, MC, B, 3, NH, NT])]
        ca_f = kept["ca_f"][:, 0:NH * CD]
        ca = [s.sb("ca0", [P, NH * CD], F32R), kept["ca1"]]
        xn = [s.sb("xn0", [P, ST, NH, DA]), kept["xn1"]]
        onehot = ca_f[:, 0:SQ]
        p1 = [kept["p1_0"]] + [s.sb(f"p1_{i}", [P, 2, CD]) for i in (1, 2)]
        raw = kept["raw"]
        rden = s.sb("tk_rden", [P, 2, KC])
        s2 = s.sb("s2", [P, B, KC, HT])
        t2 = s.sb("t2", [P, B, KC * NH])
        r2 = s.sb("r2", [P, B, KC * NH])
        p2 = s.sb("p2", [P, B, KC, 3, NH, NT])
        f_ps = [s.psum(f"f_ps{i}", [P, CH]) for i in range(2)]
        s_ps = [s.psum(f"s_ps{i}", [P, 2, CH]) for i in range(2)]
        acc_t = [s.psum(f"acc_t_ps{i}", [P, CH]) for i in range(2)]
        acc_ps = [a[0:DA, 0:CD] for a in acc_t]
        t_ps = [a[:, CD:CD + KC * (HT + 2)].rearrange("p (c n) -> p c n", c=KC) for a in acc_t]

        wqT_in, wout_in = s.sem("tk_wqT_in"), s.sem("tk_wout_in")
        tok_full, tok_done, bd_done = s.sem("tk_tok_full"), s.sem("tk_tok"), s.sem("tk_bd")
        wk2_in, wk2_full, wk2_done = s.sem("tk_wk2_in"), s.sem("tk_wk2_full"), s.sem("tk_wk2")
        vw_full, vw_hi, vw_done = s.sem("tk_vw_full"), s.sem("tk_vw_hi"), s.sem("tk_vw")
        ca_hi, ca_lo = s.sem("tk_ca_hi"), s.sem("tk_ca_lo")
        pairs = ST // 2
        xn_in = [[s.sem(f"tk_xn_in{j}") for j in range(pairs)], kept["xn1_in"]]
        oh_in = s.sem("tk_onehot_in")
        ntop_in = kept["ntop_in"]
        s_full, e_done, pv_done = s.sem("tk_s_full"), s.sem("tk_exp"), s.sem("tk_pv")
        raw_done, t_full = s.sem("tk_raw"), s.sem("tk_t_full")
        step = s.sem("tk_step")
        d2_done, e2_done, p2_done = s.sem("tk_d2"), s.sem("tk_e2"), s.sem("tk_p2")
        g_full, g_hi, g_done = s.sem("tk_g_full"), s.sem("tk_g_hi"), s.sem("tk_g_done")

        idx = gather_index()
        spans = []
        for c in range(KC):
            q = np.flatnonzero(idx // P == c)
            lo, hi = int(q[0]), int(q[-1]) + 1
            cuts = [lo, CH, hi] if lo < CH < hi else [lo, hi]
            spans += [(c, a, z) for a, z in zip(cuts, cuts[1:])]
        order = (1, 0)
        heads = [(b, h) for b in order for h in range(NH)]
        rows = lambda a: a.rearrange("(m p) n -> p m n", p=P)

        at.mx_ps = f_ps

        def maxima(k):
            k -= MAX_FROM * pairs
            return [k] if 0 <= k < MXN else []

        def folded(n):
            return 4 * (n + 1) + (n >= NH) + 2 * (n > NH)

        with nc.Block() as block:
            @block.sync
            def _(sp):
                xv = d["x_ones"].rearrange("b (t p) (h d) -> b p t h d", p=P, d=DA)

                def values(b):
                    for t in range(ST):
                        sp.dma_start(xn[b][:, t], xv[b, :, t]).then_inc(xn_in[b][t // 2], 16)

                written(sp)
                sp.dma_start(kept["wk2"][:], d["wk2_frame"]).then_inc(wk2_in, 16)
                sp.dma_start(wqT[:], rows(d["wqT"])).then_inc(wqT_in, 16)
                shift_tokens(sp, kept, ca[0], 0)
                sp.wait_ge(wk2_full, 1)
                sp.dma_start(wout[:], rows(d["wout"])).then_inc(wout_in, 16)
                at.load_a(sp, scratch, 0, 0)
                values(0)
                sp.wait_ge(ca_lo, 1)
                sp.dma_start(onehot, d["onehot"]).then_inc(oh_in, 16)
                sp.wait_ge(at.kb_ones, 1)
                at.load_b(sp, scratch, 0, 0)
                at.load_a(sp, scratch, 0, 1)
                at.shift(sp, 0, 0)

            @block.gpsimd
            def _(pool):
                written(pool)
                at.fill_ones(pool, 0)
                pool.memset(at.one[:], 1.0).then_inc(at.one_done, 1)
                pool.wait_ge(at.v_ones, 2)
                pool.wait_ge(at.one_done, 1)
                at.split_v(pool, scratch, 0, 0)

            @block.scalar
            def _(act):
                def raw_out(n):
                    act.wait_ge(pv_done, (n + 1) * pairs)
                    if n >= 2:
                        act.wait_ge(t_full, n - 1)
                    act.activation(raw[n % 2][:], acc_ps[n % 2], ACT.Copy).then_inc(raw_done, 1)

                def exp2(i):
                    b = order[i]
                    act.wait_ge(d2_done, i + 1)
                    act.activation(s2[:, b], s2[:, b], ACT.Exp, scale=SCALE).then_inc(e2_done, 1)

                def vw_out(k):
                    b, u = divmod(k, 2)
                    act.wait_ge(vw_full, k + 1)
                    act.activation(kept["vw"][:, b, u * HALF:(u + 1) * HALF], f_ps[u][0:K3, 0:HALF],
                                   ACT.Copy).then_inc(vw_hi, 1)

                def copy_gathered(i):
                    b = order[i]
                    act.wait_ge(g_full, i + 1)
                    act.activation(kept["p2g"][:, b, :], s_ps[b][0:K3].rearrange("p u n -> p (u n)"),
                                   ACT.Copy).then_inc(g_hi, 1)

                for n, (b, h) in enumerate(heads):
                    for j in range(pairs):
                        k = n * pairs + j
                        act.wait_ge(s_full, k + 1)
                        if k >= 3:
                            act.wait_ge(pv_done, k - 2)
                        act.activation(p1[k % 3][:], s_ps[k % 2][:, :, 0:CD], ACT.Exp,
                                       scale=SCALE).then_inc(e_done, 1)
                        if j == 1 and n:
                            raw_out(n - 1)
                    if n == 3:
                        act.wait_ge(kept["ca0_in"], 16)
                        act.activation(ca[0][0:K3, :], ca_f[0:K3, :], ACT.Copy).then_inc(ca_hi, 1)
                    if n == NH:
                        exp2(0)
                raw_out(len(heads) - 1)
                vw_out(0)
                copy_gathered(0)
                vw_out(1)
                exp2(1)
                vw_out(2)
                vw_out(3)
                copy_gathered(1)

            @block.vector
            def _(dve):
                steps = [0]

                def chained(ins):
                    steps[0] += 1
                    ins.then_inc(step, 1)
                    dve.wait_ge(step, steps[0])

                def fold(n):
                    b, h = heads[n]
                    dve.wait_ge(t_full, n + 1)
                    chained(dve.reciprocal(rden[:, n % 2, :], t_ps[n % 2][:, :, HT]))
                    for c in range(KC):
                        r = rden[:, n % 2, c:c + 1]
                        if h == 0:
                            chained(dve.tensor_scalar(s2[:, b, c, :], t_ps[n % 2][:, c, 0:HT], r, None, ALU.mult))
                        else:
                            chained(dve.scalar_tensor_tensor(
                                out=s2[:, b, c, :], in0=t_ps[n % 2][:, c, 0:HT], scalar=r,
                                in1=s2[:, b, c, :], op0=ALU.mult, op1=ALU.add))

                def center(b):
                    v = s2[:, b].rearrange("p c (h t) -> p (c h) t", t=NT)
                    chained(dve.tensor_reduce(t2[:, b, :], v, AX, ALU.max))
                    dve.tensor_tensor(v, v, t2[:, b, :, None].to_broadcast([P, KC * NH, NT]),
                                      ALU.subtract).then_inc(d2_done, 1)

                def weigh(i, b):
                    v = s2[:, b].rearrange("p c (h t) -> p (c h) t", t=NT)
                    dve.wait_ge(e2_done, i + 1)
                    chained(dve.tensor_reduce(t2[:, b, :], v, AX, ALU.add))
                    chained(dve.reciprocal(r2[:, b, :], t2[:, b, :]))
                    by = r2[:, b, :].rearrange("p (c h) -> p c h", c=KC)[:, :, :, None].to_broadcast([P, KC, NH, NT])
                    for r in range(3):
                        dve.tensor_tensor(p2[:, b, :, r], s2[:, b].rearrange("p c (h t) -> p c h t", t=NT), by,
                                          ALU.mult).then_inc(p2_done, 1)

                def low_vw(k):
                    b, u = divmod(k, 2)
                    dve.wait_ge(vw_hi, k + 1)
                    to = kept["vw"][HT:2 * HT, b, u * HALF:(u + 1) * HALF]
                    dve.tensor_tensor(to, f_ps[u][HT:2 * HT, 0:HALF], to.bitcast(F32),
                                      ALU.subtract).then_inc(vw_done, 1)

                def low_gathered(i):
                    dve.wait_ge(g_hi, i + 1)
                    to = kept["p2g"][2 * HT:K3, order[i], :]
                    dve.tensor_tensor(to, s_ps[order[i]][2 * HT:K3].rearrange("p u n -> p (u n)"), to.bitcast(F32),
                                      ALU.subtract).then_inc(g_done, 1)

                for i in range(2):
                    dve.wait_ge(tok_full, i + 1)
                    dve.tensor_copy(tok[i][:], f_ps[i][:, 0:MC * B * NT].rearrange("p (m t) -> p m t", m=MC)
                                    ).then_inc(tok_done, 1)
                dve.wait_ge(kept["small_in"], 64)
                dve.wait_ge(tok_done, 2)
                for i in range(2):
                    for b in range(B):
                        t = tok[i][:, :, None, b * NT:(b + 1) * NT].to_broadcast([P, MC, NH, NT])
                        own = mask[:, :, :, None].to_broadcast([P, MC, NH, NT])
                        for to in [bd[0][:, :, b]] if i == 0 else [bd[1][:, :, b, r] for r in range(3)]:
                            dve.tensor_tensor(to, t, own, ALU.mult).then_inc(bd_done, 1)
                dve.wait_ge(wk2_full, 1)
                dve.wait_ge(wk2_in, 16)
                for b in range(B):
                    dve.tensor_copy(kept["wk2"][0:D, b, :, 0:HT],
                                    f_ps[0][0:D, :].rearrange("p (h b n) -> p b h n", h=NH, b=B)[:, b]
                                    ).then_inc(wk2_done, 1)
                for k in range(len(heads) * pairs):
                    n, j = divmod(k, pairs)
                    if n == 4 and j == 0:
                        dve.wait_ge(ca_hi, 1)
                        r = slice(HT, 2 * HT)
                        dve.tensor_tensor(ca[0][r, :], ca_f[r, :], ca[0][r, :].bitcast(F32),
                                          ALU.subtract).then_inc(ca_lo, 1)
                    for m in maxima(k):
                        at.max_piece(dve, 0, 0, m)
                        if m == MXN - 1:
                            at.top(dve, 0, 0)
                    if n and j == 1:
                        fold(n - 1)
                        if n == NH:
                            center(order[0])
                        if n == NH + 1:
                            weigh(0, order[0])
                low_vw(0)
                fold(len(heads) - 1)
                center(order[1])
                low_gathered(0)
                low_vw(1)
                weigh(1, order[1])
                low_vw(2)
                low_vw(3)
                low_gathered(1)
                dve.wait_ge(g_done, B)

            @block.tensor
            def _(pe):
                def fold_tokens():
                    pe.wait_ge(kept["small_in"], 64)
                    for i, wt in enumerate((wkca, wvca)):
                        for m in range(MC):
                            for c in range(KC):
                                mm = pe.matmul(f_ps[i][:, m * B * NT:(m + 1) * B * NT], wt[:, c, m * P:(m + 1) * P],
                                               caT[:, c, :], start=c == 0, stop=c == KC - 1)
                        mm.then_inc(tok_full, 1)

                def fold_keys():
                    pe.wait_ge(wqT_in, 16)
                    pe.wait_ge(bd_done, 4 * B)
                    for h in range(NH):
                        for m in range(MC):
                            mm = pe.matmul(f_ps[0][0:D, h * B * HT:(h + 1) * B * HT], wqT[:, m, h * D:(h + 1) * D],
                                           bd[0][:, m].rearrange("p b h t -> p (b h t)"),
                                           start=m == 0, stop=m == MC - 1)
                    mm.then_inc(wk2_full, 1)

                def fold_values(b, u):
                    pe.wait_ge(wout_in, 16)
                    if b:
                        pe.wait_ge(vw_done, u + 1)
                    for m in range(MC):
                        own = bd[1][:, m, b].rearrange("p r h t -> p (r h t)")
                        mm = pe.matmul(f_ps[u][0:K3, 0:HALF], own,
                                       wout[:, m, u * HALF:(u + 1) * HALF], start=m == 0, stop=m == MC - 1)
                    mm.then_inc(vw_full, 1)

                def gather(i):
                    b = order[i]
                    pe.wait_ge(p2_done, 3 * (i + 1))
                    pe.wait_ge(e_done, total - 1 + (b == (total - 1) % 2))
                    for c, a, z in spans:
                        mm = pe.matmul(s_ps[b][0:K3, a // CH, a % CH:a % CH + z - a],
                                       p2[:, b, c].rearrange("p r h t -> p (r h t)"),
                                       onehot[:, a:z], start=True, stop=True)
                    mm.then_inc(g_full, 1)

                def scores(k):
                    n, j = divmod(k, pairs)
                    b, h = heads[n]
                    if k % (NH * pairs) == 0:
                        pe.wait_ge(ntop_in[b], 16 * NH)
                        if b == 0:
                            pe.wait_ge(ca_lo, 1)
                    if k >= 2:
                        pe.wait_ge(e_done, k - 1)
                    for t in range(2):
                        st = 2 * j + t
                        mm = pe.matmul(s_ps[k % 2][:, t, 0:CD],
                                       kept["u"][0:K3 + 1, b * SQ + st * P:b * SQ + (st + 1) * P],
                                       ca[b][0:K3 + 1, h * CD:(h + 1) * CD], start=True, stop=True)
                    mm.then_inc(s_full, 1)

                def token_scores(n):
                    b, h = heads[n]
                    if n == 0:
                        pe.wait_ge(wk2_done, B)
                    pe.wait_ge(raw_done, n + 1)
                    for c in range(KC):
                        mm = pe.matmul(t_ps[n % 2][:, c, :], raw[n % 2][:, c * P:(c + 1) * P],
                                       kept["wk2"][:, b, h, :], start=True, stop=True)
                    mm.then_inc(t_full, 1)

                pe.wait_ge(kept["u_ones"], 1)
                total = len(heads) * pairs
                scores(0)
                for k in range(total):
                    n, j = divmod(k, pairs)
                    b, h = heads[n]
                    if k + 1 < total:
                        scores(k + 1)
                    if n == 0 or (b == 0 and h == 0):
                        pe.wait_ge(xn_in[b][j], 32)
                    pe.wait_ge(e_done, k + 1)
                    if j == 0 and n >= 2:
                        pe.wait_ge(raw_done, n - 1)
                        pe.wait_ge(step, folded(n - 2))
                    for t in range(2):
                        mm = pe.matmul(acc_ps[n % 2], xn[b][:, 2 * j + t, h, :], p1[k % 3][:, t, :],
                                       start=j == 0 and t == 0, stop=j == pairs - 1 and t == 1)
                    mm.then_inc(pv_done, 1)
                    for m in maxima(k):
                        if m == 0:
                            pe.wait_ge(wk2_done, B)
                        at.score_piece(pe, 0, 0, m)
                    if k == 3:
                        fold_tokens()
                    if k == 5:
                        fold_keys()
                    if j == 1 and n:
                        token_scores(n - 1)
                pe.wait_ge(oh_in, 16)
                pe.wait_ge(at.mx_done, MXN)
                fold_values(0, 0)
                token_scores(len(heads) - 1)
                gather(0)
                fold_values(0, 1)
                fold_values(1, 0)
                fold_values(1, 1)
                gather(1)


def attend(nc, kept, at, wout, d, scratch):
    with ExitStack() as stack:
        s = Scope(nc, stack)
        at.second(s)
        ka, kb, qa, qb, v_s, o_raw = at.ka, at.kb, at.qa, at.qb, at.v_s, at.o_raw
        wout_f = kept["ca_f"][:].rearrange("p (m n) -> p m n", m=MC)
        prob = kept["probs"] + [s.sb("prob_last", [P, SQ])]
        ph = [s.sb(f"prob_hi{i}", [P, SQ], F32R) for i in range(PB)]
        pl = [s.sb(f"prob_lo{i}", [P, SQ], F32R) for i in range(PB)]
        s_ps = [s.psum(f"at_s_ps{i}", [P, SQ]) for i in range(2)]
        o_ps = s.psum("at_o_ps", [DA, SQ])
        at.mx_ps = [s.psum(f"at_mx_ps{i}", [P, CH]) for i in range(2)]

        s_full, e_done, ph_done = s.sem("at_s_full"), s.sem("at_exp"), s.sem("at_ph")
        pl_dve, pl_pool = s.sem("at_pl_dve"), s.sem("at_pl_pool")
        pv_done = s.sem("at_pv")
        o_ones = s.sem("at_o_ones")
        wout_in, wout_hi, wout_lo = s.sem("at_wout_in"), s.sem("at_wout_hi"), s.sem("at_wout_lo")

        STEPS = 2 * KT
        LASTP = G // 2 - 1
        keys = lambda t: P if t < KT - 1 else LASTK

        def wait_low(eng, i, j):
            mine = [k % KT in POOL_T for k in range(STEPS)]
            if mine[j]:
                eng.wait_ge(pl_pool, i * mine.count(True) + mine[:j + 1].count(True))
            else:
                eng.wait_ge(pl_dve, i * mine.count(False) + mine[:j + 1].count(False))

        def make_low(eng, i, j, sem):
            n, r = i * STEPS + j, keys(j % KT)
            eng.wait_ge(ph_done, n + 1)
            eng.tensor_tensor(pl[j % PB][0:r, :], prob[j % PF][0:r, :], ph[j % PB][0:r, :].bitcast(F32),
                              ALU.subtract).then_inc(sem, 1)

        def both(eng, body):
            with eng.Fori(0, LASTP) as i:
                body(i, False)
            body(LASTP, True)

        with nc.Block() as block:
            @block.sync
            def _(sp):
                def finish(i, p):
                    at.spread(sp, scratch, i, p)
                    at.put(sp, scratch, 2 * i + p, p)

                def body(i, last):
                    at.shift(sp, i, 1)
                    if not last:
                        sp.wait_ge(s_full, (2 * i + 1) * KT)
                        at.load_a(sp, scratch, i + 1, 0)
                        at.load_b(sp, scratch, i + 1, 0)
                    finish(i, 0)
                    if not last:
                        at.shift(sp, i + 1, 0)
                        sp.wait_ge(s_full, (2 * i + 2) * KT)
                        at.load_a(sp, scratch, i + 1, 1)
                        at.load_b(sp, scratch, i + 1, 1)
                        finish(i, 1)

                sp.wait_ge(at.kb_ones, 2)
                at.load_b(sp, scratch, 0, 1)
                sp.dma_start(wout_f, d["wout"].rearrange("(m p) n -> p m n", p=P)).then_inc(wout_in, 16)
                both(sp, body)
                sp.wait_ge(at.hs_out[0], 16 + 16 * G // 2)
                sp.wait_ge(at.hs_out[1], 16 + 16 * (G // 2 - 1))

            @block.gpsimd
            def _(pool):
                def split_wout(k):
                    m, low = divmod(k, 2)
                    hi, lo = wout
                    if low:
                        pool.wait_ge(wout_hi, m + 1)
                        pool.tensor_tensor(lo[:, m, :], wout_f[:, m, :], hi[:, m, :].bitcast(F32),
                                           ALU.subtract).then_inc(wout_lo, 1)
                    else:
                        pool.wait_ge(wout_in, 16)
                        pool.tensor_tensor(hi[:, m, :], wout_f[:, m, :], at.one[:].to_broadcast([P, HID]),
                                           ALU.mult).then_inc(wout_hi, 1)

                def body(i, last):
                    for j in range(STEPS):
                        p, t = divmod(j, KT)
                        if last and p == 0 and 5 <= t < 5 + 2 * MC:
                            split_wout(t - 5)
                        if t + 1 in POOL_T:
                            make_low(pool, i, j + 1, pl_pool)
                        if p == 1 and t == 8 and not last:
                            pool.wait_ge(pv_done, PB + (2 * i + 1) * KT)
                            at.split_v(pool, scratch, i + 1, 0)
                        if p == 1 and t == 12:
                            at.normalise(pool, 2 * i, 0)
                        if p == 0 and t == 8:
                            pool.wait_ge(pv_done, PB + 2 * i * KT)
                            at.split_v(pool, scratch, i, 1)
                        if p == 0 and t == 12:
                            at.normalise(pool, 2 * i - 1, 1)

                at.fill_ones(pool, 1)
                pool.wait_ge(at.v_ones, 4)
                pool.memset(at.rbc[:], 1.0).then_inc(at.rbc_in, 16)
                pool.memset(o_raw[1][0:D, :], 1.0).then_inc(o_ones, 1)
                pool.wait_ge(at.rbc_in, 16)
                pool.wait_ge(o_ones, 1)
                both(pool, body)
                pool.wait_ge(wout_lo, MC)

            @block.scalar
            def _(act):
                def exp(i, j, before=None, between=lambda: None):
                    n, r = i * STEPS + j, keys(j % KT)
                    act.wait_ge(s_full, n + 1)
                    if j >= PF:
                        wait_low(act, i, j - PF)
                    elif before is not None:
                        wait_low(act, before, j - PF + STEPS)
                    act.activation(prob[j % PF][0:r, :], s_ps[j % 2][0:r, :], ACT.Exp, scale=SCALE
                                   ).then_inc(e_done, 1)
                    between()
                    act.wait_ge(e_done, n + 1)
                    act.wait_ge(pv_done, n + 1)
                    act.activation(ph[j % PB][0:r, :], prob[j % PF][0:r, :], ACT.Copy).then_inc(ph_done, 1)

                def take(i, p):
                    g = 2 * i + p
                    act.wait_ge(pv_done, PB + (g + 1) * KT)
                    act.wait_ge(at.hs_out[p], (i + 1) * 16)
                    act.activation(o_raw[p][:], o_ps[:], ACT.Copy).then_inc(at.o_act, 1)

                def body(i, last):
                    for j in range(STEPS):
                        ends = j % KT == KT - 1
                        between = (lambda: take(i, j // KT)) if ends else (lambda: None)
                        if j + 2 < STEPS:
                            exp(i, j + 2, between=between)
                        elif not last:
                            exp(i + 1, j + 2 - STEPS, i, between)
                        else:
                            between()

                act.sem_inc(at.o_act, 1)
                for p in range(2):
                    act.sem_inc(at.hs_out[p], 16)
                exp(0, 0)
                exp(0, 1)
                both(act, body)

            @block.vector
            def _(dve):
                def split(i, j):
                    if j % KT not in POOL_T:
                        make_low(dve, i, j, pl_dve)

                def body(i, last):
                    for j in range(STEPS):
                        p, t = divmod(j, KT)
                        todo = [] if last and p else list(pieces(t))
                        for k in todo[:SPLIT_AT]:
                            at.max_piece(dve, i + p, 1 - p, k)
                        if j + 1 < STEPS:
                            split(i, j + 1)
                        elif not last:
                            split(i + 1, 0)
                        for k in todo[SPLIT_AT:]:
                            at.max_piece(dve, i + p, 1 - p, k)
                        if todo and todo[-1] == MXN - 1:
                            at.top(dve, i + p, 1 - p)
                        if j == 3:
                            at.invert(dve, 1, i + 1)
                        if j == KT + 3:
                            at.invert(dve, 0, i + 1)

                dve.memset(at.den[1][:], 1.0).then_inc(at.den_in[1], 16)
                split(0, 0)
                both(dve, body)

            @block.tensor
            def _(pe):
                def scores(i, j, between):
                    n = i * STEPS + j
                    p, t = divmod(j, KT)
                    r = keys(t)
                    if t == 0:
                        pe.wait_ge(at.qk_in[p], (i + 1) * 64)
                        pe.wait_ge(at.qkb_in[p], (i + 1) * 64)
                        pe.wait_ge(at.neg_in[p], (i + 1) * 16)
                    if not (isinstance(i, int) and i == 0 and j < 2):
                        pe.wait_ge(e_done, n - 1)
                    for a, y, first in ((ka[p], qa[p], True), (kb[p], qb[p], False)):
                        rows = P if first else SHIFT + 1
                        for u in range(2):
                            mm = pe.matmul(s_ps[j % 2][0:r, u * CH:(u + 1) * CH], a[0:rows, t * P:t * P + r],
                                           y[0:rows, u * CH:(u + 1) * CH], start=first, stop=not first)
                        if first:
                            between()
                    mm.then_inc(s_full, 1)

                def values(i, j, between):
                    n = i * STEPS + j
                    p, t = divmod(j, KT)
                    r = keys(t)
                    if t == 0:
                        pe.wait_ge(at.v_split, 2 * i + p + 1)
                        pe.wait_ge(at.o_act, 2 * i + p + 1)
                    wait_low(pe, i, j)
                    hi, lo = v_s[p]
                    for m, (a, y) in enumerate(((hi, ph), (lo, ph), (hi, pl))):
                        for u in range(2):
                            mm = pe.matmul(o_ps[:, u * CH:(u + 1) * CH], a[0:r, t, :],
                                           y[j % PB][0:r, u * CH:(u + 1) * CH],
                                           start=t == 0 and m == 0, stop=t == KT - 1 and m == 2)
                        if m < 2:
                            between()
                    mm.then_inc(pv_done, 1)

                def body(i, last):
                    for j in range(STEPS):
                        p, t = divmod(j, KT)
                        todo = [] if last and p else list(pieces(t))

                        def between():
                            if todo:
                                at.score_piece(pe, i + p, 1 - p, todo.pop(0))

                        if j + 2 < STEPS:
                            scores(i, j + 2, between)
                        elif not last:
                            scores(i + 1, j + 2 - STEPS, between)
                        values(i, j, between)
                        assert not todo

                pe.sem_inc(pv_done, PB)
                pe.wait_ge(at.kb_ones, 1)
                pe.wait_ge(at.v_ones, 2)
                for j in range(2):
                    scores(0, j, lambda: None)
                both(pe, body)


def pieces(t):
    assert sum(PIECES) == MXN
    return range(sum(PIECES[:t]), sum(PIECES[:t + 1]))


def output(nc, kept, at, wout, d, scratch, out):
    with ExitStack() as stack:
        s = Scope(nc, stack)
        bias = s.sb("o_bias", [P, HID])
        p2 = [s.sb(f"o_p2_{p}", [K3, P], F32R) for p in range(2)]
        hs_f = [s.sb(f"o_hs_f{p}", [P, MC, P]) for p in range(2)]
        hs_s = [(s.sb(f"o_hs_hi{p}", [P, MC, P], F32R), s.sb(f"o_hs_lo{p}", [P, MC, P], F32R)) for p in range(2)]
        x_t = [s.sb(f"o_x{p}", [P, HID]) for p in range(2)]
        o_t = [s.sb(f"o_o{p}", [P, HID]) for p in range(2)]
        ps = [s.psum(f"o_ps{p}", [P, 2, CH]) for p in range(2)]

        bias_in = s.sem("o_bias_in")
        hs_in = [s.sem(f"o_hs_in{p}") for p in range(2)]
        x_in = [s.sem(f"o_x_in{p}") for p in range(2)]
        p2_in = [s.sem(f"o_p2_in{p}") for p in range(2)]
        hi, lo = s.sem("o_hi"), s.sem("o_lo")
        xb, full = s.sem("o_xb"), s.sem("o_full")
        done = s.sem("o_done")
        o_out = [s.sem(f"o_out{p}") for p in range(2)]
        C = 2
        hs_v = scratch["hs"].rearrange("(b m p) q -> b p m q", m=MC, p=P)
        PAIRS = ST // 2

        def pairs(eng, body, first=lambda: None, second=lambda: None):
            body(0, 0, False)
            first()
            with eng.Fori(1, PAIRS) as i:
                body(0, i, False)
            second()
            with eng.Fori(0, PAIRS - 1) as i:
                body(1, i, False)
            body(1, PAIRS - 1, True)

        with nc.Block() as block:
            @block.sync
            def _(sp):
                def body(b, i, last):
                    for p in range(2):
                        n = b * ST + 2 * i + p
                        q = bass.ds((2 * i + p) * P, P)
                        sp.wait_ge(lo, n + 1)
                        sp.dma_start(hs_f[p][:], hs_v[b, :, :, q]).then_inc(hs_in[p], 16)
                        sp.wait_ge(done, n + 1)
                        sp.dma_start(x_t[p][:], d["x"][b, q, :]).then_inc(x_in[p], 16)
                        sp.dma_start(p2[p][:].bitcast(F32), kept["p2g"][:, b, q].bitcast(F32)).then_inc(p2_in[p], 16)
                        if isinstance(i, int) and b == 0 and p == 0:
                            sp.dma_start(bias[:], d["bias"].to_broadcast([P, HID])).then_inc(bias_in, 16)

                def put():
                    at.put(sp, scratch, G - 1, 1)
                    sp.wait_ge(at.hs_out[1], 16 + 16 * G // 2)

                pairs(sp, body, lambda: at.spread(sp, scratch, G // 2 - 1, 1), put)

            @block.gpsimd
            def _(pool):
                def body(b, i, last):
                    for p in range(2):
                        pool.wait_ge(x_in[p], (b * PAIRS + i + 1) * 16)
                        pool.tensor_tensor(x_t[p][:], x_t[p][:], bias[:], ALU.add).then_inc(xb, 1)

                pool.wait_ge(bias_in, 16)
                pairs(pool, body, lambda: at.normalise(pool, G - 1, 1))

            @block.scalar
            def _(act):
                def split(b, i, p):
                    act.wait_ge(hs_in[p], (b * PAIRS + i + 1) * 16)
                    act.wait_ge(full, b * ST + 2 * i + p + 1)
                    act.activation(hs_s[p][0][:], hs_f[p][:], ACT.Copy).then_inc(hi, 1)

                def body(b, i, last):
                    for p in range(2):
                        n = b * ST + 2 * i + p
                        if p == 0:
                            split(b, i, 1)
                        elif not last:
                            split(b, i + 1, 0)
                        act.wait_ge(done, n + 1 + C)
                        act.dma_start(out[bass.ds(n * P, P), :], o_t[p][:]).then_inc(o_out[p], 16)

                for p in range(2):
                    act.sem_inc(o_out[p], 16)
                split(0, 0, 0)
                pairs(act, body)
                for p in range(2):
                    act.wait_ge(o_out[p], 16 + 16 * B * PAIRS)

            @block.vector
            def _(dve):
                def split(n, p):
                    dve.wait_ge(hi, n + 1)
                    dve.tensor_tensor(hs_s[p][1][:], hs_f[p][:], hs_s[p][0][:].bitcast(F32),
                                      ALU.subtract).then_inc(lo, 1)

                def body(b, i, last):
                    for p in range(2):
                        n = b * ST + 2 * i + p
                        if not (last and p):
                            split(n + 1, 1 - p)
                        if isinstance(i, int) and b == 0 and p == 0:
                            at.invert(dve, 1, G // 2 + 1)
                        dve.wait_ge(full, n + 1 + C)
                        dve.wait_ge(xb, n + 1)
                        dve.wait_ge(o_out[p], (b * PAIRS + i + 1) * 16)
                        u = lambda a: a.rearrange("p (u n) -> p u n", u=2)
                        dve.tensor_tensor(u(o_t[p][:]), ps[p][:, :, 0:HALF], u(x_t[p][:]), ALU.add).then_inc(done, 1)

                dve.sem_inc(lo, C)
                dve.sem_inc(done, C)
                split(0, 0)
                pairs(dve, body)

            @block.tensor
            def _(pe):
                def body(b, i, last):
                    for p in range(2):
                        n = b * ST + 2 * i + p
                        pe.wait_ge(lo, n + 1 + C)
                        pe.wait_ge(done, n + 1)
                        for m in range(MC):
                            for k, (a, y) in enumerate(products(hs_s[p], wout)):
                                for u in range(2):
                                    pe.matmul(ps[p][:, u, 0:HALF], a[:, m, :], y[:, m, u * HALF:(u + 1) * HALF],
                                              start=m == 0 and k == 0, stop=False)
                        pe.wait_ge(p2_in[p], (b * PAIRS + i + 1) * 16)
                        for u in range(2):
                            mm = pe.matmul(ps[p][:, u, 0:HALF], p2[p][:], kept["vw"][:, b, u * HALF:(u + 1) * HALF],
                                           start=False, stop=True)
                        mm.then_inc(full, 1)

                pe.sem_inc(full, C)
                pairs(pe, body)


def program(nc, d, out):
    dram = lambda name, shape: nc.dram_tensor(name, shape, F32, kind="Internal").ap()
    scratch = {
        "kh": dram("k_hi_d", [B * HID, SKV]), "kl": dram("k_lo_d", [B * HID, SKV]),
        "qh": dram("q_hi_d", [B * HID, SQ]), "ql": dram("q_lo_d", [B * HID, SQ]),
        "v": dram("v_d", [G, P, KT * D]), "hs": dram("heads_d", [B * HID, SQ]), "rden": dram("rden_d", [G, SQ]),
    }
    with ExitStack() as stack:
        s = Scope(nc, stack)
        kept = {
            "u": s.sb("u", [3 * HT + 1, B * SQ], F32R),
            "u_ones": s.sem("u_ones"),
            "x_f": s.sb("x_f", [P, 1, MC, CH]),
            "ca_f": s.sb("ca_f", [P, MC * HID]),
            "small_in": s.sem("small_in"),
            "ca0_in": s.sem("ca0_in"),
            "xn1_in": [s.sem(f"xn1_in{j}") for j in range(ST // 2)],
            "ntop_in": [s.sem(f"ntop_in{b}") for b in range(B)],
            "ntop": s.sb("ntop", [P, B, NH * KC], F32R),
        }
        wq_store = s.place_before("wq_store", [P, 2, MC, HID], F32R)
        wq_flat = s.sb("wq_place", [P, 2 * MC * HID])
        kept["ca1"] = s.place_before("ca1", [P, NH * CD], F32R)
        probs = s.sb("probs", [P, PF - 1, SQ])
        assert (PF - 1) * SQ == NH * CD
        kept["probs"] = [probs[:, i] for i in range(PF - 1)]
        x_flat = kept["x_f"][:].rearrange("p o m n -> p (o m n)")
        n_x, n_k, n_p = ST * NH * DA, KC * HID, 2 * CD
        n_c, n_m = KC * B * NT, MC * NH
        blocks = lambda a, m: a.rearrange("p (m n) -> p m n", m=m)
        kept["xn1"] = wq_flat[:, 0:n_x].rearrange("p (t h d) -> p t h d", t=ST, h=NH)
        kept["p1_0"] = blocks(wq_flat[:, n_x:n_x + n_p], 2)
        kept["wkca"] = blocks(x_flat[:, 0:n_k], KC)
        kept["caT"] = blocks(x_flat[:, n_k:n_k + n_c], KC)
        kept["mask"] = blocks(x_flat[:, n_k + n_c:n_k + n_c + n_m], MC)
        kept["x_hi"] = s.place_before("x_hi", [P, MC, CH], F32R)
        x_hi_flat = s.sb("x_hi_place", [P, MC * CH])
        kept["wvca"] = blocks(x_hi_flat[:, 0:n_k], KC)
        kept["raw"] = [x_flat[0:DA, n_k + n_c + n_m:n_k + n_c + n_m + CD], x_hi_flat[0:DA, n_k:n_k + CD]]
        with ExitStack() as inner:
            ws = Scope(nc, inner)
            pair = lambda n, k, c: (ws.sb(f"{n}_hi", [P, k, c], F32R), ws.sb(f"{n}_lo", [P, k, c], F32R))
            ring = [(ws.sb(f"out_hi{i}", [P, CH], F32R), ws.sb(f"out_lo{i}", [P, CH], F32R)) for i in range(RING)]
            v_t = ws.sb("v_t", [P, 2, NH, CH // P, D])
            w = {"ring": ring, "v_t": v_t, "wq": (wq_store[:, 0], wq_store[:, 1]), "wk": pair("wk", KC, HID),
                 "wv": pair("wv", KC, HID), "wqca": pair("wqca", MC, K3)}
            written = project(nc, s, kept, w, d, scratch)
        kept |= {
            "wk2": s.sb("wk2", [DA, B, NH, HT + 2]),
            "vw": s.sb("vw", [K3, B, HID], F32R),
            "p2g": s.sb("p2g", [K3, B, SQ], F32R),
        }
        at = Heads(s, x_flat, x_hi_flat)
        tokens(nc, kept, at, written, d, scratch)
        wout = w["wq"]
        attend(nc, kept, at, wout, d, scratch)
        output(nc, kept, at, wout, d, scratch, out.rearrange("b s n -> (b s) n"))


def layouts(x, ctx, Wq, Wk, Wv, Wq_ca, Wk_ca, Wv_ca, Wout, b_out):
    ca = ctx[:, SK:, :]
    wqca = np.zeros((NH, D, 3, NH, NT), Wq_ca.dtype)
    ca_bd = np.zeros((B, 3, NH, NT, NH, CD), ctx.dtype)
    for h in range(NH):
        for r in range(3):
            wqca[h, :, r, h, :] = Wq_ca[:, h * D:(h + 1) * D].T
            ca_bd[:, r, h, :, h, :] = ca
    mask = np.zeros((NH, D, NH), np.float32)
    for h in range(NH):
        mask[h, :, h] = 1
    frame = np.zeros((DA, B, NH, HT + 2), np.float32)
    frame[D, :, :, HT] = 1
    x_ones = np.ones((B, SQ, NH, DA), x.dtype)
    x_ones[:, :, :, 0:D] = x.reshape(B, SQ, NH, D)
    onehot = np.zeros((P, SQ), np.float32)
    onehot[gather_index() % P, np.arange(SQ)] = 1
    return {
        "x": x, "x_ones": x_ones.reshape(B, SQ, NH * DA), "xT": x.transpose(0, 2, 1), "ctxT": ctx.transpose(0, 2, 1),
        "wq": Wq, "wqT": Wq.T, "wk": Wk, "wv": Wv, "wkca": Wk_ca, "wvca": Wv_ca, "wout": Wout,
        "bias": b_out.reshape(1, HID), "caT": ca.transpose(2, 0, 1).reshape(CD, B * NT),
        "wqca": wqca.reshape(HID, 3 * HT), "caBD": ca_bd.reshape(B, 3 * HT, NH * CD),
        "mask": mask.reshape(HID, NH), "wk2_frame": frame, "onehot": onehot,
    }


def kernel(x, ctx_768, L0_xattn_Wq, L0_xattn_Wk, L0_xattn_Wv, L0_xattn_Wq_ca, L0_xattn_Wk_ca,
           L0_xattn_Wv_ca, L0_xattn_Wout, L0_xattn_b_out):
    import concourse.bacc as bacc
    from concourse.bass_utils import run_bass_kernel_spmd

    a = [np.asarray(v) for v in (x, ctx_768, L0_xattn_Wq, L0_xattn_Wk, L0_xattn_Wv, L0_xattn_Wq_ca,
                                 L0_xattn_Wk_ca, L0_xattn_Wv_ca, L0_xattn_Wout, L0_xattn_b_out)]
    nc = bacc.Bacc("TRN2", target_bir_lowering=False, num_devices=1)
    arrays, d = {}, {}
    for name, v in layouts(*a).items():
        arrays[f"in_{name}"] = np.ascontiguousarray(v)
        d[name] = nc.dram_tensor(f"in_{name}", v.shape, mybir.dt.from_np(v.dtype), kind="ExternalInput").ap()
    out = nc.dram_tensor("out", (B, SQ, HID), F32, kind="ExternalOutput").ap()
    program(nc, d, out)
    r = run_bass_kernel_spmd(nc, [arrays], core_ids=[0])
    return r.results[0]["out"]
```
